# Optimizing a Trainium2 kernel written in Bass

```python
import numpy as np
import jax
import jax.numpy as jnp

def _softmax(x, axis=-1):
    return jax.nn.softmax(x, axis=axis)

def _gelu(x):
    return jax.nn.gelu(x, approximate=True)

def _silu(x):
    return jax.nn.silu(x)

def _sigmoid(x):
    return jax.nn.sigmoid(x)

def _layernorm(x, axis=-1, eps=1e-05):
    m = jnp.mean(x, axis=axis, keepdims=True)
    v = jnp.var(x, axis=axis, keepdims=True)
    return (x - m) / jnp.sqrt(v + eps)

def _scatter_add(tgt, idx, src, axis=0):
    return tgt.at[idx].add(src)

def _segment_sum(src, seg, n):
    return jax.ops.segment_sum(src, seg, n)
kernel_name = 'mk_recurrent_d1_jaxref_r4_18acc3'

def setup_inputs(seed: int=0):
    np.random.seed(seed)
    _w = jnp.asarray

    def _L0_attn_setup():
        import jax, jax.numpy as jnp
        import numpy as np
        B, T, V, D = (4, 512, 512, 128)
        key = jax.random.key(seed)
        ks = jax.random.split(key, 8)
        x = jax.random.normal(ks[0], (B, T, V), dtype=jnp.float32)
        Wq = 0.02 * jax.random.normal(ks[1], (V, D), dtype=jnp.float32)
        Wk = 0.02 * jax.random.normal(ks[2], (3, V, D), dtype=jnp.float32)
        Wv = 0.02 * jax.random.normal(ks[3], (3, V, D), dtype=jnp.float32)
        Wo = 0.02 * jax.random.normal(ks[4], (D, V), dtype=jnp.float32)
        Wg = 0.02 * jax.random.normal(ks[5], (V, 3), dtype=jnp.float32)
        decay_logits = jnp.array([0.0, 3.0, 5.0], dtype=jnp.float32)
        out_scale = jnp.float32(0.1)
        return {'x': x, 'Wq': Wq, 'Wk': Wk, 'Wv': Wv, 'Wo': Wo, 'Wg': Wg, 'decay_logits': decay_logits, 'out_scale': out_scale}
    _L0_attn_in = _L0_attn_setup()

    def _L0_ffn_setup():
        import jax, jax.numpy as jnp
        import numpy as np
        HIDDEN = 512
        INTER = 1376
        LUT_SIZE = 16

        def _ghost_linear(x, idx, lut):
            w = lut[idx]
            return jnp.einsum('bsh,oh->bso', x, w)
        key = jax.random.key(seed)
        k_x, k_lut, k_g, k_u, k_d = jax.random.split(key, 5)
        x = jax.random.normal(k_x, (2, 1024, HIDDEN), dtype=jnp.float32)
        lut = jax.random.normal(k_lut, (LUT_SIZE,), dtype=jnp.float32) * 0.02
        gate_idx = jax.random.randint(k_g, (INTER, HIDDEN), 0, LUT_SIZE, dtype=jnp.int32)
        up_idx = jax.random.randint(k_u, (INTER, HIDDEN), 0, LUT_SIZE, dtype=jnp.int32)
        down_idx = jax.random.randint(k_d, (HIDDEN, INTER), 0, LUT_SIZE, dtype=jnp.int32)
        return {'x': x, 'lut': lut, 'gate_idx': gate_idx, 'up_idx': up_idx, 'down_idx': down_idx}
    _L0_ffn_in = _L0_ffn_setup()
    _d = {'L0_attn_x': _L0_attn_in['x'], 'L0_attn_Wq': _L0_attn_in['Wq'], 'L0_attn_Wk': _L0_attn_in['Wk'], 'L0_attn_Wv': _L0_attn_in['Wv'], 'L0_attn_Wo': _L0_attn_in['Wo'], 'L0_attn_Wg': _L0_attn_in['Wg'], 'L0_attn_decay_logits': _L0_attn_in['decay_logits'], 'L0_attn_out_scale': _L0_attn_in['out_scale'], 'L0_ffn_lut': _L0_ffn_in['lut'], 'L0_ffn_gate_idx': _L0_ffn_in['gate_idx'], 'L0_ffn_up_idx': _L0_ffn_in['up_idx'], 'L0_ffn_down_idx': _L0_ffn_in['down_idx']}
    _x0 = _d['L0_attn_x']
    _d['L0_attn_x'] = jax.random.normal(jax.random.fold_in(jax.random.key(seed), 1), (8, 1024, 512), dtype=_x0.dtype)
    del _x0
    return _d

def reference(L0_attn_x, L0_attn_Wq, L0_attn_Wk, L0_attn_Wv, L0_attn_Wo, L0_attn_Wg, L0_attn_decay_logits, L0_attn_out_scale, L0_ffn_lut, L0_ffn_gate_idx, L0_ffn_up_idx, L0_ffn_down_idx):

    def _L0_attn_ref(x, Wq, Wk, Wv, Wo, Wg, decay_logits, out_scale):
        import jax, jax.numpy as jnp
        import numpy as np
        B, T, V, D = (4, 512, 512, 128)
        Tn = x.shape[1]
        q = x @ Wq
        gate = jax.nn.softmax(x @ Wg, axis=-1)
        pos = jnp.arange(Tn)
        diff = pos[None, :] - pos[:, None]
        causal = (diff > 0).astype(x.dtype)
        expn = jnp.maximum(diff - 1, 0).astype(x.dtype)
        blended = jnp.zeros(q.shape, dtype=x.dtype)
        for i in range(3):
            k = x @ Wk[i]
            v = x @ Wv[i]
            decay = jax.nn.sigmoid(decay_logits[i])
            w = decay ** expn * causal
            scores = jnp.einsum('btd,bsd->bts', q, k) * w[None]
            retrieved = jnp.einsum('bts,bsd->btd', scores, v)
            blended = blended + gate[..., i:i + 1] * retrieved
        return blended @ Wo * out_scale

    def _L0_ffn_ref(x, lut, gate_idx, up_idx, down_idx):
        import jax, jax.numpy as jnp
        import numpy as np
        HIDDEN = 512
        INTER = 1376
        LUT_SIZE = 16

        def _ghost_linear(x, idx, lut):
            w = lut[idx]
            return jnp.einsum('bsh,oh->bso', x, w)
        gate = _ghost_linear(x, gate_idx, lut)
        up = _ghost_linear(x, up_idx, lut)
        h = jax.nn.silu(gate) * up
        return _ghost_linear(h, down_idx, lut)
    x = L0_attn_x
    xn = _layernorm(x, axis=-1)
    s = _L0_attn_ref(xn, L0_attn_Wq, L0_attn_Wk, L0_attn_Wv, L0_attn_Wo, L0_attn_Wg, L0_attn_decay_logits, L0_attn_out_scale)
    g = _silu(_L0_ffn_ref(xn, L0_ffn_lut, L0_ffn_gate_idx, L0_ffn_up_idx, L0_ffn_down_idx))
    x = x + s * g
    return x

_drawn_inputs = setup_inputs


def setup_inputs(seed=0):
    import zlib

    import numpy as np

    out = dict(_drawn_inputs(seed))
    spreads = {}
    factors = {}
    for name, (base, spread) in spreads.items():
        noise = np.random.default_rng([zlib.crc32(name.encode()), seed]).standard_normal(out[name].shape)
        drawn = base * np.exp(spread * noise) if base else spread * noise
        out[name] = jnp.asarray(drawn.astype(out[name].dtype))
    for name, factor in factors.items():
        out[name] = (out[name] * factor).astype(out[name].dtype)
    return out
```

```python
from contextlib import ExitStack

import concourse.bass as bass
from concourse import mybir

ALU = mybir.AluOpType
ACT = mybir.ActivationFunctionType
AX = mybir.AxisListType
F32 = mybir.dt.float32
F16 = mybir.dt.float16
I32 = mybir.dt.int32
RMAX = bass.bass_isa.ReduceOp.max

P = 128
BANK = 512
GT = 4
GRP = GT * P
NLUT = 16
CG = 4
QR = P // CG

XP = 10
WP = 8
HP = -(5 + 2 * WP + XP)


def attention_ffn_kernel(nc, x, idx, lut, wq, wk, wv, wo, wg, decay_logits, out_scale, out):
    NTOK, V = x.shape
    D = wq.shape[1]
    NH = wk.shape[0]
    KC = V // P
    F = 1376
    FC = -(-F // P)
    FM = [min(P, F - m * P) for m in range(FC)]
    T = 1024
    NB = NTOK // T
    GPB = T // GRP
    assert GPB == 2 and KC == 4 and D == P and V == BANK and NH == 3
    NBLK = idx.shape[0]
    W_UP, W_DOWN = KC * F, 2 * KC * F
    UNR = 3
    assert NBLK % UNR == 0 and NBLK * BANK >= W_DOWN + FC * V
    QKV = (1 + 2 * NH) * D + NH
    CK, CV, CGT = D, (1 + NH) * D, (1 + 2 * NH) * D
    HD = NH * D

    with ExitStack() as ctx:
        def sb(name, shape, dt):
            return ctx.enter_context(nc.sbuf_tensor(name, shape, dt))

        def ps(name, dt=F32):
            return ctx.enter_context(nc.psum_tensor(name, [P, BANK], dt))

        def sem(name):
            return ctx.enter_context(nc.semaphore(name))

        w_hi = sb("w_hi", [P, NBLK * BANK], F16)
        w_lo = sb("w_lo", [P, NBLK * BANK], F16)
        a_hi = sb("a_hi", [P, KC, QKV], F16)
        a_lo = sb("a_lo", [P, KC, QKV], F16)
        wo_sb = sb("wo_sb", [P, V], F32)
        x_sb = sb("x_sb", [P, 2, GT, V], F32)
        xhat = sb("xhat", [P, GT, V], F32)
        xt_hi = sb("xt_hi", [P, 2, KC, GRP], F16)
        xt_lo = sb("xt_lo", [P, 2, KC, GRP], F16)
        n_qk, n_v = (1 + NH) * GRP, GT * HD
        attn = sb("attn", [P, n_qk + 2 * n_v], F32)
        qk = attn[:, 0:n_qk].rearrange("p (j t) -> p j t", j=1 + NH)
        v_sb = attn[:, n_qk:n_qk + n_v].rearrange("p (t c) -> p t c", t=GT)
        vb_sb = attn[:, n_qk + n_v:n_qk + 2 * n_v].rearrange("p (t c) -> p t c", t=GT)
        state = sb("state", [P, HD], F32)
        faded = sb("faded", [P, HD], F32)
        mixed = sb("mixed", [P, 2, D], F32)
        ident = sb("ident", [P, P], F32)
        mask = sb("mask", [P, NH, P], F32)
        mask_up = faded[:, :].rearrange("p (h t) -> p h t", h=NH)
        fade_s = sb("fade_s", [P, NH], F32)
        flip = sb("flip", [P, P], F32)
        fade_end = sb("fade_end", [NH, P], F32)
        fade_rows = nc.dram_tensor("fade_rows", [NH, 2 * P], F32, kind="Internal")
        fade_t = sb("fade_t", [P, NH], F32)
        fade_tile = sb("fade_tile", [P, NH], F32)
        decay = sb("decay", [P, NH], F32)
        dlog = sb("dlog", [P, NH], F32)
        oscale = sb("oscale", [P, 1], F32)
        nhalf = sb("nhalf", [P, GT], F32)
        amax = sb("amax", [P, 5], F32)
        gmax = sb("gmax", [P, 5], F32)
        ebits = sb("ebits", [P, 5], I32)
        up_e = sb("up_e", [P, 5], I32)
        down_e = sb("down_e", [P, 5], I32)
        hf_e = sb("hf_e", [P, 2], I32)
        scale_up = sb("scale_up", [P, 5], I32)
        scale_down = sb("scale_down", [P, 5], I32)
        scale_hf = sb("scale_hf", [P, 2], I32)
        stats = sb("stats", [P, GT, 6], F32)
        moments = sb("moments", [P, GT, 2], F32)
        var = sb("var", [P, GT], F32)
        rstd = sb("rstd", [P, GT], F32)
        logit = sb("logit", [P, GT, NH], F32)
        lmax = sb("lmax", [P, GT], F32)
        lsub = sb("lsub", [P, GT, NH], F32)
        lth = sb("lth", [P, GT, NH], F32)
        lnum = sb("lnum", [P, GT, NH], F32)
        lden = sb("lden", [P, GT, NH], F32)
        lrec = sb("lrec", [P, GT, NH], F32)
        lexp = sb("lexp", [P, GT, NH], F32)
        lsum = sb("lsum", [P, GT], F32)
        lrs = sb("lrs", [P, GT], F32)
        gate = sb("gate", [P, GT, NH], F32)
        gate_t = sb("gate_t", [P, GT, NH], F32)
        lutrow = sb("lutrow", [P, NLUT], F32)
        lutcol = sb("lutcol", [P, CG], F32)
        lut_sc = sb("lut_sc", [P, CG], F32)
        lut_hi = sb("lut_hi", [P, CG], F16)
        lut_hi32 = sb("lut_hi32", [P, CG], F32)
        lut_lo32 = sb("lut_lo32", [P, CG], F32)
        pidx = sb("pidx", [P, 1], I32)
        pquad = sb("pquad", [P, 1], I32)
        code = sb("code", [P, CG], F32)
        eye4 = sb("eye4", [P, CG, QR], F32)
        eye = sb("eye", [P, QR], F32)
        pick_hi = sb("pick_hi", [P, CG, QR], F16)
        pick_lo = sb("pick_lo", [P, CG, QR], F16)

        HB = FC * GRP * 2
        sizes = dict(h_hi=HB, h_lo=HB, sg=2 * 2048, h32=2 * 2048, g=2 * 2048, y1=2 * 2048, y=GT * 2048,
                     bl=GRP * 4, kn=2 * HD * 4, pr=2 * HD * 4)
        build = UNR * CG * CG * BANK * 2
        region = sb("region", [P, max(sum(sizes.values()), build) // 4], F32)
        at = {}
        pos = 0
        for k, n in sizes.items():
            at[k] = region[:, pos // 4:(pos + n) // 4]
            pos += n
        h_hi = at["h_hi"].bitcast(F16).rearrange("p (m t) -> p m t", m=FC)
        h_lo = at["h_lo"].bitcast(F16).rearrange("p (m t) -> p m t", m=FC)
        sg = at["sg"].rearrange("p (b t) -> p b t", b=2)
        h32 = at["h32"].rearrange("p (b t) -> p b t", b=2)
        g_sb = at["g"].rearrange("p (b t) -> p b t", b=2)
        y1 = at["y1"].rearrange("p (b t) -> p b t", b=2)
        y_sb = at["y"].rearrange("p (b t) -> p b t", b=GT)
        blend_t = at["bl"].rearrange("p (b t) -> p b t", b=GT)
        k_nat = at["kn"].rearrange("p (b t) -> p b t", b=2)
        probs = at["pr"].rearrange("p (b h t) -> p b h t", b=2, h=NH)
        n_oh = UNR * CG * CG * BANK // 2
        onehot = region[:, 0:n_oh].bitcast(F16).rearrange("p (u j q c) -> p u j q c", u=UNR, j=CG, q=CG)
        a32 = attn[:, 0:KC * QKV].rearrange("p (k c) -> p k c", k=KC)
        n_ix = CG * BANK // 2
        spare = x_sb[:, 1].rearrange("p t v -> p (t v)")
        codes = [c.bitcast(F16).rearrange("p (q c) -> p q c", q=CG)
                 for c in (attn[:, KC * QKV:KC * QKV + n_ix], spare[:, 0:n_ix], spare[:, n_ix:2 * n_ix])]

        G = [ps("G0"), ps("G1")]
        U = [ps("U0"), ps("U1")]
        B = [ps("B0"), ps("B1"), ps("B2"), ps("B3")]
        LUHI = [G[0], G[1], B[0]]
        LULO = [U[0], U[1], B[1]]

        s_x = [sem("x_in0"), sem("x_in1")]
        s_y = [sem(f"y_out{t}") for t in range(GT)]
        s_idx = [sem(f"codes_in{u}") for u in range(UNR)]
        s_w = sem("qkv_in")
        s_wo = sem("wo_in")
        s_small = sem("small_in")
        s_const = sem("const_ready")
        s_cstep = sem("const_step")
        s_init = sem("init_step")
        s_amax = sem("amax_ready")
        s_gmax = sem("gmax_ready")
        s_scale = sem("scales_ready")
        s_dec = sem("decay_step")
        s_pow = sem("power_step")
        s_pick = sem("pick_ready")
        s_row = sem("fade_rows_written")
        s_mrow = sem("mask_rows_in")
        s_pmask = sem("mask_in_psum")
        s_mask = sem("mask_ready")
        s_lhi = sem("lut_step")
        s_ahi = sem("a_hi_ready")
        s_alo = sem("a_lo_ready")
        s_oh = sem("onehot_ready")
        s_lu = sem("lookup_done")
        s_wst = sem("w_stored")
        s_bn = sem("bn_done")
        s_mv = sem("moments_done")
        s_var = sem("var_done")
        s_rstd = sem("rstd_done")
        s_xh = sem("xhat_ready")
        s_xt = sem("xt_in_psum")
        s_xhi = sem("xt_hi_ready")
        s_xlo = sem("xt_lo_ready")
        s_pqk = sem("qk_in_psum")
        s_qk = sem("qk_ready")
        s_pv = sem("v_in_psum")
        s_v = sem("v_ready")
        s_lg = sem("logits_ready")
        s_vb = sem("vb_ready")
        s_sm = sem("softmax_step")
        s_th = sem("tanh_ready")
        s_pkn = sem("k_nat_in_psum")
        s_kn = sem("k_nat_ready")
        s_psc = sem("scores_in_psum")
        s_pr = sem("probs_ready")
        s_pat = sem("retrieved_in_psum")
        s_mix = sem("mix_step")
        s_pu = sem("update_in_psum")
        s_fade = sem("state_faded")
        s_st = sem("state_ready")
        s_pbl = sem("blend_in_psum")
        s_bl = sem("blend_ready")
        s_pg = sem("gate_in_psum")
        s_pup = sem("up_in_psum")
        s_sg = sem("silu_ready")
        s_h = sem("h_ready")
        s_hhi = sem("h_hi_ready")
        s_hlo = sem("h_lo_ready")
        s_pf = sem("ffn_in_psum")
        s_pso = sem("attn_in_psum")
        s_g = sem("g_ready")
        s_y1 = sem("product_ready")
        s_yr = sem("y_ready")

        x_v = x.rearrange("(n t p) v -> n p t v", t=GT, p=P)
        out_v = out.rearrange("(n t p) v -> n p t v", t=GT, p=P)

        f_up = scale_up[:, :].bitcast(F32)
        f_down = scale_down[:, :].bitcast(F32)
        f_hf = scale_hf[:, :].bitcast(F32)

        SCORES = {0: 3, 2: 2, 4: 1, 6: 0}
        RETRIEVE = {1: 3, 3: 2, 5: 1, 7: 0}
        BLEND = {2: 3, 4: 2, 6: 1, 8: 0}
        NEXT_T = {2: 0, 4: 1, 6: 2, 8: 3}
        PARTS = ((0, CK), (CK, CV), (CV, CGT), (CGT, QKV))
        NSM = 10
        NMIX = 2 * NH

        FREE = 1

        def row_group(i, g):
            return i * GPB + (GPB - 1 - g)

        block = ctx.enter_context(nc.Block())

        @block.sync
        def _(sp):
            for t in range(GT):
                sp.sem_inc(s_y[t], 16 * FREE)
            sp.dma_start(lutrow[:, :], lut.partition_broadcast(P)).then_inc(s_small, 16)
            for c in range(CG):
                src = lut.rearrange("(j c) -> c j", c=CG)[c]
                sp.dma_start(lutcol[QR * c:QR * (c + 1), :], src.partition_broadcast(QR),
                             allow_slow_non_contiguous=True).then_inc(s_small, 16)
            sp.dma_start(dlog[:, :], decay_logits.partition_broadcast(P)).then_inc(s_small, 16)
            sp.dma_start(oscale[:, :], out_scale.partition_broadcast(P)).then_inc(s_small, 16)
            sp.dma_start(x_sb[:, 0], x_v[row_group(0, 0)]).then_inc(s_x[0], 16)
            sp.dma_start(a32[:, :, 0:D], wq.rearrange("(c p) d -> p c d", p=P)).then_inc(s_w, 16)
            for h in range(NH):
                sp.dma_start(a32[:, :, CK + h * D:CK + (h + 1) * D],
                             wk[h].rearrange("(c p) d -> p c d", p=P)).then_inc(s_w, 16)
                sp.dma_start(a32[:, :, CV + h * D:CV + (h + 1) * D],
                             wv[h].rearrange("(c p) d -> p c d", p=P)).then_inc(s_w, 16)
            sp.dma_start(a32[:, :, CGT:QKV], wg.rearrange("(c p) d -> p c d", p=P)).then_inc(s_w, 16)
            sp.dma_start(wo_sb[:, :], wo).then_inc(s_wo, 16)

            with nc.allow_non_contiguous_dma(reason="384 values, once"):
                sp.wait_ge(s_cstep, 5)
                sp.dma_start(fade_rows[:, P:2 * P], fade_end[:, :]).then_inc(s_row, 16)
                sp.wait_ge(s_pow, 1)
                sp.dma_start(fade_rows[:, 0:P].rearrange("h t -> t h"), fade_t[:, :]).then_inc(s_row, 16)
                sp.wait_ge(s_row, 32)
                sp.dma_start(mask_up[:, :, :], bass.AP(fade_rows, 1, [[1, P], [2 * P, NH], [1, P]])).then_inc(s_mrow, 16)
            sp.wait_ge(s_oh, CG * NBLK)

            def group(i, g, last):
                gi = i * GPB + g
                if not last:
                    sp.wait_ge(s_yr, gi * GT + FREE)
                    nxt = row_group(i + (g + 1) // GPB, (g + 1) % GPB)
                    sp.dma_start(x_sb[:, 1 - g], x_v[nxt]).then_inc(s_x[1 - g], 16)
                for t in range(GT):
                    sp.wait_ge(s_yr, gi * GT + t + 1 + FREE)
                    sp.dma_start(out_v[row_group(i, g)][:, t], y_sb[:, t]).then_inc(s_y[t], 16)

            with sp.Fori(0, NB - 1) as i:
                for g in range(GPB):
                    group(i, g, False)
            for g in range(GPB):
                group(NB - 1, g, g == GPB - 1)
            for t in range(GT):
                sp.wait_ge(s_y[t], 16 * (NB * GPB + FREE))

        @block.gpsimd
        def _(pool):
            def load_codes(b):
                u = b % UNR
                if b >= UNR:
                    pool.wait_ge(s_oh, CG * (b - UNR + 1))
                rows = idx[b].rearrange("p q c -> p (q c)").unsqueeze(0).broadcast_to([CG, QR, CG * BANK])
                pool.dma_start(codes[u].rearrange("p q c -> p (q c)"), rows).then_inc(s_idx[u], 16)

            for b in range(UNR):
                load_codes(b)
            nc.gpsimd.iota(pidx[:, :], pattern=[[0, 1]], base=0, channel_multiplier=1).then_inc(s_const, 1)
            nc.gpsimd.memset(eye4[:, :, :], 0.0).then_inc(s_cstep, 1)
            nc.gpsimd.memset(ident[:, :], 0.0).then_inc(s_cstep, 1)
            nc.gpsimd.memset(flip[:, :], 0.0).then_inc(s_cstep, 1)
            nc.gpsimd.memset(nhalf[:, :], -0.5).then_inc(s_cstep, 1)
            nc.gpsimd.memset(fade_end[:, :], 0.0).then_inc(s_cstep, 1)
            pool.wait_ge(s_cstep, 5)
            nc.gpsimd.affine_select(out=eye4[:, :, :], in_=eye4[:, :, :], compare_op=ALU.not_equal, fill=1.0, base=0,
                                    pattern=[[-QR, CG], [-1, QR]], channel_multiplier=1).then_inc(s_const, 1)
            nc.gpsimd.affine_select(out=ident[:, :], in_=ident[:, :], compare_op=ALU.not_equal, fill=1.0, base=0,
                                    pattern=[[-1, P]], channel_multiplier=1).then_inc(s_const, 1)
            nc.gpsimd.affine_select(out=flip[:, :], in_=flip[:, :], compare_op=ALU.not_equal, fill=1.0,
                                    base=-(P - 1), pattern=[[1, P]], channel_multiplier=1).then_inc(s_const, 1)
            pool.wait_ge(s_amax, 5)
            nc.gpsimd.partition_all_reduce(gmax[:, 0:5], amax[:, 0:5], P, RMAX).then_inc(s_gmax, 1)

            pool.wait_ge(s_var, 2)
            nc.gpsimd.tensor_tensor(rstd[:, :], var[:, :], nhalf[:, :], ALU.pow).then_inc(s_rstd, 1)
            for b in range(UNR, 2 * UNR):
                load_codes(b)
            for b in range(2 * UNR, NBLK):
                load_codes(b)
            nc.gpsimd.iota(fade_s[:, :], pattern=[[0, NH]], base=0, channel_multiplier=1,
                           allow_small_or_imprecise_dtypes=True).then_inc(s_cstep, 1)
            nc.gpsimd.iota(fade_t[:, :], pattern=[[0, NH]], base=P - 1, channel_multiplier=-1,
                           allow_small_or_imprecise_dtypes=True).then_inc(s_cstep, 1)
            nc.gpsimd.memset(fade_tile[:, :], float(P)).then_inc(s_cstep, 1)
            pool.wait_ge(s_dec, 3)
            pool.wait_ge(s_cstep, 8)
            for m in (fade_t, fade_s, fade_tile):
                nc.gpsimd.tensor_tensor(m[:, :], decay[:, :], m[:, :], ALU.pow).then_inc(s_pow, 1)
            pool.wait_ge(s_scale, 3)
            for n, (a, b) in enumerate(PARTS):
                pool.wait_ge(s_ahi, 2 * n + 2)
                nc.gpsimd.tensor_tensor(a_lo[:, :, a:b], a32[:, :, a:b], a_hi[:, :, a:b],
                                        ALU.subtract).then_inc(s_alo, 1)

            def group(i, g):
                gi = i * GPB + g
                pool.wait_ge(s_var, 2 * gi + 4)
                nc.gpsimd.tensor_tensor(rstd[:, :], var[:, :], nhalf[:, :], ALU.pow).then_inc(s_rstd, 1)

            with pool.Fori(0, NB - 1) as i:
                for g in range(GPB):
                    group(i, g)
            group(NB - 1, 0)

        @block.scalar
        def _(act):
            act.sem_inc(s_g, FREE)
            act.sem_inc(s_bl, FREE)
            act.wait_ge(s_small, 16 * (CG + 3))
            nc.scalar.activation(decay[:, :], dlog[:, :], ACT.Exp, scale=-1.0).then_inc(s_dec, 1)

            def xt_high(par, t, n):
                act.wait_ge(s_xt, n)
                nc.scalar.activation(xt_hi[:, par, :, t * P:(t + 1) * P],
                                     B[2][:, :].rearrange("p (k c) -> p k c", k=KC), ACT.Copy).then_inc(s_xhi, 1)

            for t in range(GT):
                xt_high(0, t, t + 1)

            def a_high():
                act.wait_ge(s_w, 16 * (2 + 2 * NH))
                act.wait_ge(s_scale, 3)
                for n, (a, b) in enumerate(PARTS):
                    nc.scalar.activation(a32[:, :, a:b], a32[:, :, a:b], ACT.Copy,
                                         scale=f_up[:, n:n + 1]).then_inc(s_ahi, 1)
                    act.wait_ge(s_ahi, 2 * n + 1)
                    nc.scalar.activation(a_hi[:, :, a:b], a32[:, :, a:b], ACT.Copy).then_inc(s_ahi, 1)

            def store(i, u):
                b = i * UNR + u
                col = bass.ds(b * BANK, BANK)
                act.wait_ge(s_lu, b + 1)
                nc.scalar.activation(w_hi[:, col], LUHI[u][:, :], ACT.Copy).then_inc(s_wst, 1)
                nc.scalar.activation(w_lo[:, col], LULO[u][:, :], ACT.Copy).then_inc(s_wst, 1)

            with act.Fori(0, NBLK // UNR) as i:
                for u in range(UNR):
                    store(i, u)
            a_high()
            act.wait_ge(s_pmask, 1)
            nc.scalar.activation(mask[:, :, :].rearrange("p h t -> p (h t)"), B[3][:, 0:HD], ACT.Copy).then_inc(s_mask, 1)

            def group(i, g, last):
                gi = i * GPB + g
                for j in range(1 + NH):
                    act.wait_ge(s_pqk, gi * (1 + NH) + j + 1)
                    n = min(j, 1)
                    nc.scalar.activation(qk[:, j], B[j % 2][:, :], ACT.Copy,
                                         scale=f_down[:, n:n + 1]).then_inc(s_qk, 1)
                for t in range(GT):
                    act.wait_ge(s_pv, gi * GT + t + 1)
                    nc.scalar.activation(v_sb[:, t], B[2 + t % 2][:, 0:HD], ACT.Copy,
                                         scale=f_down[:, 2:3]).then_inc(s_v, 1)
                    nc.scalar.activation(logit[:, t], B[2 + t % 2][:, HD:HD + NH], ACT.Copy,
                                         scale=f_down[:, 3:4]).then_inc(s_lg, 1)
                act.wait_ge(s_sm, gi * NSM + 2)
                nc.scalar.activation(lth[:, :, :], lsub[:, :, :], ACT.Tanh, scale=0.5).then_inc(s_th, 1)
                for m in range(FC):
                    M = FM[m]
                    act.wait_ge(s_pg, gi * FC + m + 1)
                    if m >= 2:
                        act.wait_ge(s_h, gi * FC + m - 1)
                    nc.scalar.activation(sg[0:M, m % 2], G[m % 2][0:M, :], ACT.Silu,
                                         scale=f_down[0:M, 4:5]).then_inc(s_sg, 1)
                    act.wait_ge(s_h, gi * FC + m + 1)
                    nc.scalar.activation(h_hi[0:M, m], h32[0:M, m % 2], ACT.Copy).then_inc(s_hhi, 1)
                    if m in SCORES:
                        n = m // 2
                        act.wait_ge(s_pkn, gi * GT + n + 1)
                        nc.scalar.activation(k_nat[:, n % 2], B[0][:, 0:HD], ACT.Copy).then_inc(s_kn, 1)
                    if m in NEXT_T and not last:
                        xt_high(1 - g, NEXT_T[m], gi * GT + GT + NEXT_T[m] + 1)
                    if m in BLEND:
                        act.wait_ge(s_pbl, gi * GT + m // 2)
                        nc.scalar.activation(blend_t[:, BLEND[m]], B[3][:, 0:P], ACT.Copy).then_inc(s_bl, 1)
                for t in range(GT):
                    act.wait_ge(s_pf, gi * GT + t + 1)
                    if t >= 2:
                        act.wait_ge(s_y1, gi * GT + t - 1 + FREE)
                    nc.scalar.activation(g_sb[:, t % 2], G[(t + 1) % 2][:, :], ACT.Silu,
                                         scale=f_hf[:, 1:2]).then_inc(s_g, 1)

            with act.Fori(0, NB - 1) as i:
                for g in range(GPB):
                    group(i, g, False)
            for g in range(GPB):
                group(NB - 1, g, g == GPB - 1)

        @block.vector
        def _(dve):
            V_ = nc.vector
            dve.sem_inc(s_y1, FREE)
            dve.sem_inc(s_yr, FREE)
            init = [0]

            def step(ins):
                init[0] += 1
                ins.then_inc(s_init, 1)
                dve.wait_ge(s_init, init[0])

            def norm(par, loads, gi, t0=0):
                def aggregate(t):
                    V_.bn_aggr(moments[:, t], stats[:, t]).then_inc(s_mv, 1)

                def variance(a, b):
                    V_.tensor_scalar(var[:, a:b], moments[:, a:b, 1], 1e-5, 2.0 ** (-2 * XP), ALU.add,
                                     ALU.mult).then_inc(s_var, 1)

                n0 = gi * GT
                dve.wait_ge(s_x[par], loads)
                for t in range(GT):
                    if t >= 2:
                        dve.wait_ge(s_bn, n0 + t - 1)
                    V_.bn_stats(stats[:, t], x_sb[:, par, t]).then_inc(s_bn, 1)
                    if t >= 2:
                        aggregate(t - 2)
                dve.wait_ge(s_bn, n0 + GT)
                dve.wait_ge(s_mv, n0 + 2)
                variance(0, 2)
                aggregate(2)
                aggregate(3)
                dve.wait_ge(s_mv, n0 + GT)
                variance(2, 4)

            def xhat_tile(par, gi, t):
                if t == 0:
                    dve.wait_ge(s_rstd, gi + 1)
                V_.tensor_scalar(xhat[:, t], x_sb[:, par, t], moments[:, t, 0:1], rstd[:, t:t + 1],
                                 ALU.subtract, ALU.mult).then_inc(s_xh, 1)

            def xt_low(par, t, n):
                dve.wait_ge(s_xhi, n)
                V_.tensor_tensor(xt_lo[:, par, :, t * P:(t + 1) * P],
                                 B[2][:, :].rearrange("p (k c) -> p k c", k=KC),
                                 xt_hi[:, par, :, t * P:(t + 1) * P], ALU.subtract).then_inc(s_xlo, 1)

            def compare(i, u, first):
                b = i * UNR + u
                dve.wait_ge(s_idx[u], 16 * i + 16)
                if not first:
                    dve.wait_ge(s_lu, b - UNR + 1)
                for j in range(CG):
                    V_.tensor_scalar(onehot[:, u, j], codes[u], code[:, j:j + 1], None,
                                     ALU.is_equal).then_inc(s_oh, 1)

            dve.wait_ge(s_const, 1)
            step(V_.tensor_scalar(pquad[:, :], pidx[:, :], 5, None, ALU.logical_shift_right))
            for j in range(CG):
                ins = V_.tensor_scalar(code[:, j:j + 1], pquad[:, :], float(CG * j), None, ALU.add)
                ins.then_inc(s_init, 1)
                init[0] += 1
            dve.wait_ge(s_init, init[0])

            dve.wait_ge(s_small, 16 * (CG + 3))
            V_.tensor_reduce(amax[:, 4:5], lutrow[:, :], AX.X, ALU.max, apply_absolute_value=True).then_inc(s_amax, 1)
            dve.wait_ge(s_w, 16 * (2 + 2 * NH))
            for n, (a, b) in enumerate(PARTS):
                V_.tensor_reduce(amax[:, n:n + 1], a32[:, :, a:b], AX.XY, ALU.max,
                                 apply_absolute_value=True).then_inc(s_amax, 1)
            dve.wait_ge(s_dec, 1)
            V_.tensor_scalar(decay[:, :], decay[:, :], 1.0, None, ALU.add).then_inc(s_dec, 1)
            dve.wait_ge(s_dec, 2)
            V_.reciprocal(decay[:, :], decay[:, :]).then_inc(s_dec, 1)
            norm(0, 16, 0)
            for u in range(UNR):
                compare(0, u, True)

            dve.wait_ge(s_gmax, 1)
            step(V_.tensor_scalar(ebits[:, :], gmax[:, :].bitcast(I32), 23, None, ALU.logical_shift_right))
            step(V_.tensor_scalar(ebits[:, 0:4], ebits[:, 0:4], 40.0, 200.0, ALU.max, ALU.min))
            step(V_.tensor_scalar(ebits[:, 4:5], ebits[:, 4:5], 90.0, 165.0, ALU.max, ALU.min))
            step(V_.tensor_scalar(up_e[:, :], ebits[:, :], -1.0, 254.0 + WP, ALU.mult, ALU.add))
            step(V_.tensor_scalar(down_e[:, :], ebits[:, :], float(-WP - XP), None, ALU.add))
            step(V_.tensor_scalar(hf_e[:, 0:1], ebits[:, 4:5], -1.0, 254.0 + WP + HP, ALU.mult, ALU.add))
            step(V_.tensor_scalar(hf_e[:, 1:2], ebits[:, 4:5], 3.0, 127.0 - 3 * 127 - 3 * WP - XP - HP,
                                  ALU.mult, ALU.add))
            V_.tensor_scalar(scale_up[:, :], up_e[:, :], 23, None, ALU.logical_shift_left).then_inc(s_scale, 1)
            V_.tensor_scalar(scale_down[:, :], down_e[:, :], 23, None, ALU.logical_shift_left).then_inc(s_scale, 1)
            V_.tensor_scalar(scale_hf[:, :], hf_e[:, :], 23, None, ALU.logical_shift_left).then_inc(s_scale, 1)
            dve.wait_ge(s_scale, 3)

            step(V_.tensor_scalar(lut_sc[:, :], lutcol[:, :], f_up[:, 4:5], None, ALU.mult))
            step(V_.tensor_copy(lut_hi[:, :], lut_sc[:, :]))
            step(V_.tensor_copy(lut_hi32[:, :], lut_hi[:, :]))
            step(V_.tensor_tensor(lut_lo32[:, :], lut_sc[:, :], lut_hi32[:, :], ALU.subtract))
            dve.wait_ge(s_const, 3)
            step(V_.tensor_reduce(eye[:, :], eye4[:, :, :].rearrange("p a c -> p c a"), AX.X, ALU.add))
            for j in range(CG):
                V_.tensor_scalar(pick_hi[:, j], eye[:, :], lut_hi32[:, j:j + 1], None, ALU.mult).then_inc(s_pick, 1)
                V_.tensor_scalar(pick_lo[:, j], eye[:, :], lut_lo32[:, j:j + 1], None, ALU.mult).then_inc(s_pick, 1)

            for t in range(GT):
                xhat_tile(0, 0, t)
            for t in range(GT):
                xt_low(0, t, t + 1)

            with dve.Fori(1, NBLK // UNR) as i:
                for u in range(UNR):
                    compare(i, u, False)

            def heads(ap):
                return ap.rearrange("p (h c) -> p h c", h=NH)

            def spread(col):
                return col[:, :].unsqueeze(2).broadcast_to([P, NH, P])

            def softmax(gi):
                n0 = gi * NSM
                wide = lambda ap: ap[:, :].unsqueeze(2).broadcast_to([P, GT, NH])
                dve.wait_ge(s_lg, gi * GT + GT)
                V_.tensor_reduce(lmax[:, :], logit[:, :, :], AX.X, ALU.max).then_inc(s_sm, 1)
                dve.wait_ge(s_sm, n0 + 1)
                V_.tensor_tensor(lsub[:, :, :], logit[:, :, :], wide(lmax), ALU.subtract).then_inc(s_sm, 1)
                dve.wait_ge(s_th, gi + 1)
                V_.tensor_scalar(lnum[:, :, :], lth[:, :, :], 1.0, None, ALU.add).then_inc(s_sm, 1)
                V_.tensor_scalar(lden[:, :, :], lth[:, :, :], -1.0, 1.0, ALU.mult, ALU.add).then_inc(s_sm, 1)
                dve.wait_ge(s_sm, n0 + 4)
                V_.reciprocal(lrec[:, :, :], lden[:, :, :]).then_inc(s_sm, 1)
                dve.wait_ge(s_sm, n0 + 5)
                V_.tensor_tensor(lexp[:, :, :], lnum[:, :, :], lrec[:, :, :], ALU.mult).then_inc(s_sm, 1)
                dve.wait_ge(s_sm, n0 + 6)
                V_.tensor_reduce(lsum[:, :], lexp[:, :, :], AX.X, ALU.add).then_inc(s_sm, 1)
                dve.wait_ge(s_sm, n0 + 7)
                V_.reciprocal(lrs[:, :], lsum[:, :]).then_inc(s_sm, 1)
                dve.wait_ge(s_sm, n0 + 8)
                V_.tensor_tensor(gate[:, :, :], lexp[:, :, :], wide(lrs), ALU.mult).then_inc(s_sm, 1)
                dve.wait_ge(s_sm, n0 + 9)
                V_.tensor_tensor(gate_t[:, :, :], gate[:, :, :],
                                 fade_t[:, :].unsqueeze(1).broadcast_to([P, GT, NH]), ALU.mult).then_inc(s_sm, 1)

            def mix(gi, g, n, t):
                c0 = (gi * GT + n) * NMIX
                dve.wait_ge(s_pat, gi * GT + n + 1)
                if n == 0:
                    dve.wait_ge(s_sm, gi * NSM + NSM)
                acc = mixed[:, n % 2]
                V_.tensor_scalar(acc, B[3][:, 0:D], gate[:, t, 0:1], None, ALU.mult).then_inc(s_mix, 1)
                for h in range(1, NH):
                    dve.wait_ge(s_mix, c0 + h)
                    V_.scalar_tensor_tensor(out=acc, in0=B[3][:, h * D:(h + 1) * D], scalar=gate[:, t, h:h + 1],
                                            in1=acc, op0=ALU.mult, op1=ALU.add).then_inc(s_mix, 1)
                for h in range(NH):
                    dve.wait_ge(s_mix, c0 + NH + h)
                    V_.scalar_tensor_tensor(out=acc, in0=B[2][:, h * D:(h + 1) * D], scalar=gate_t[:, t, h:h + 1],
                                            in1=acc, op0=ALU.mult, op1=ALU.add).then_inc(s_mix, 1)

            def update_state(i, g, n):
                if n == GT - 1 and g == GPB - 1:
                    dve.wait_ge(s_pat, (i * GPB + g) * GT + n + 1)
                    V_.memset(state[:, :], 0.0).then_inc(s_st, 1)
                    return
                k = i * (GPB * GT - 1) + g * GT + n
                dve.wait_ge(s_st, i * GPB * GT + g * GT + n + 1)
                V_.tensor_tensor(heads(faded[:, :]), heads(state[:, :]), spread(fade_tile), ALU.mult).then_inc(s_fade, 1)
                dve.wait_ge(s_fade, k + 1)
                dve.wait_ge(s_pu, k + 1)
                V_.tensor_tensor(state[:, :], B[0][:, 0:HD], faded[:, :], ALU.add).then_inc(s_st, 1)

            def group(i, g, last):
                gi = i * GPB + g
                for t in range(GT):
                    dve.wait_ge(s_v, gi * GT + t + 1)
                    V_.tensor_tensor(heads(vb_sb[:, t]), heads(v_sb[:, t]), spread(fade_s), ALU.mult).then_inc(s_vb, 1)
                softmax(gi)
                if not last:
                    norm(1 - g, 16 * (i + g) + 16, gi + 1)
                    for t in range(GT):
                        xhat_tile(1 - g, gi + 1, t)

                def low(m):
                    M = FM[m]
                    dve.wait_ge(s_hhi, gi * FC + m + 1)
                    V_.tensor_tensor(h_lo[0:M, m], h32[0:M, m % 2], h_hi[0:M, m], ALU.subtract).then_inc(s_hlo, 1)

                for m in range(FC):
                    M = FM[m]
                    dve.wait_ge(s_sg, gi * FC + m + 1)
                    dve.wait_ge(s_pup, gi * FC + m + 1)
                    if m >= 2:
                        dve.wait_ge(s_hlo, gi * FC + m - 1)
                    V_.scalar_tensor_tensor(out=h32[0:M, m % 2], in0=sg[0:M, m % 2], scalar=f_hf[0:M, 0:1],
                                            in1=U[m % 2][0:M, :], op0=ALU.mult, op1=ALU.mult).then_inc(s_h, 1)
                    if m:
                        low(m - 1)
                    if m in SCORES:
                        n = m // 2
                        dve.wait_ge(s_psc, gi * GT + n + 1)
                        V_.tensor_tensor(probs[:, n % 2].rearrange("p h c -> p (h c)"), B[1][:, 0:HD],
                                         mask[:, :, :].rearrange("p h c -> p (h c)"), ALU.mult).then_inc(s_pr, 1)
                    if m in NEXT_T and not last:
                        xt_low(1 - g, NEXT_T[m], gi * GT + GT + NEXT_T[m] + 1)
                    if m in RETRIEVE:
                        mix(gi, g, m // 2, RETRIEVE[m])
                        update_state(i, g, m // 2)
                low(FC - 1)
                for t in range(GT):
                    dve.wait_ge(s_g, gi * GT + t + 1 + FREE)
                    dve.wait_ge(s_pso, gi * GT + t + 1)
                    dve.wait_ge(s_yr, gi * GT + max(t - 1, 0) + FREE)
                    V_.scalar_tensor_tensor(out=y1[:, t % 2], in0=U[(t + 1) % 2][:, :], scalar=oscale[:, 0:1],
                                            in1=g_sb[:, t % 2], op0=ALU.mult, op1=ALU.mult).then_inc(s_y1, 1)
                    dve.wait_ge(s_y1, gi * GT + t + 1 + FREE)
                    dve.wait_ge(s_y[t], 16 * (gi + FREE))
                    V_.tensor_tensor(y_sb[:, t], y1[:, t % 2], x_sb[:, g, t], ALU.add).then_inc(s_yr, 1)

            dve.wait_ge(s_pow, 3)
            dve.wait_ge(s_mask, 1)
            V_.memset(state[:, :], 0.0).then_inc(s_st, 1)
            with dve.Fori(0, NB - 1) as i:
                for g in range(GPB):
                    group(i, g, False)
            for g in range(GPB):
                group(NB - 1, g, g == GPB - 1)

        @block.tensor
        def _(pe):
            T_ = nc.tensor

            def x_transposes(t, n):
                pe.wait_ge(s_xh, n)
                for k in range(KC):
                    ins = T_.transpose(B[2][:, k * P:(k + 1) * P], xhat[:, t, k * P:(k + 1) * P], ident[:, :])
                ins.then_inc(s_xt, 1)

            pe.wait_ge(s_const, 4)
            for t in range(GT):
                if t:
                    pe.wait_ge(s_xlo, t)
                x_transposes(t, t + 1)

            def look_up(i, u, first):
                b = i * UNR + u
                if not first:
                    pe.wait_ge(s_wst, 2 * (b - UNR + 1))
                for j in range(CG):
                    pe.wait_ge(s_oh, b * CG + j + 1)
                    for pick, bank in ((pick_hi, LUHI[u]), (pick_lo, LULO[u])):
                        for q in range(CG):
                            ins = T_.matmul(bank[QR * q:QR * (q + 1), :], pick[:, j], onehot[:, u, j, q],
                                            start=(j == 0), stop=(j == CG - 1))
                ins.then_inc(s_lu, 1)

            pe.wait_ge(s_pick, 2 * CG)
            for u in range(UNR):
                look_up(0, u, True)
            with pe.Fori(1, NBLK // UNR) as i:
                for u in range(UNR):
                    look_up(i, u, False)

            def three(bank, pairs, cols, M=P):
                n = 0
                for k, (sh, sl, mh, ml) in enumerate(pairs):
                    for a, b in ((sh, mh), (sh, ml), (sl, mh)):
                        ins = T_.matmul(bank[0:M, 0:cols], a, b, start=(n == 0), stop=(n == 3 * len(pairs) - 1))
                        n += 1
                return ins

            def scores(gi, g, n, t):
                cols = slice(t * P, (t + 1) * P)
                if n == 0:
                    pe.wait_ge(s_qk, gi * (1 + NH) + 1 + NH)
                else:
                    pe.wait_ge(s_st, gi * GT + n + 1)
                for h in range(NH):
                    ins = T_.transpose(B[0][:, h * D:(h + 1) * D], qk[:, 1 + h, cols], ident[:, :])
                ins.then_inc(s_pkn, 1)
                if n:
                    pe.wait_ge(s_pr, gi * GT + n)
                for h in range(NH):
                    ins = T_.matmul(B[1][:, h * D:(h + 1) * D], qk[:, 1 + h, cols], qk[:, 0, cols],
                                    start=True, stop=True)
                ins.then_inc(s_psc, 1)

            def retrieve(i, g, n, t):
                gi = i * GPB + g
                cols = slice(t * P, (t + 1) * P)
                pe.wait_ge(s_st, gi * GT + n + 1)
                T_.matmul(B[2][:, 0:HD], qk[:, 0, cols], state[:, :], start=True, stop=True)
                pe.wait_ge(s_pr, gi * GT + n + 1)
                if n == 0:
                    pe.wait_ge(s_v, gi * GT + GT)
                for h in range(NH):
                    ins = T_.matmul(B[3][:, h * D:(h + 1) * D], probs[:, n % 2, h], v_sb[:, t, h * D:(h + 1) * D],
                                    start=True, stop=True)
                ins.then_inc(s_pat, 1)
                if n == GT - 1 and g == GPB - 1:
                    return
                pe.wait_ge(s_kn, gi * GT + n + 1)
                if n == 0:
                    pe.wait_ge(s_vb, gi * GT + GT)
                for h in range(NH):
                    ins = T_.matmul(B[0][:, h * D:(h + 1) * D], k_nat[:, n % 2, h * D:(h + 1) * D],
                                    vb_sb[:, t, h * D:(h + 1) * D], start=True, stop=True)
                ins.then_inc(s_pu, 1)

            def blend(gi, n):
                pe.wait_ge(s_mix, (gi * GT + n + 1) * NMIX)
                T_.transpose(B[3][:, 0:P], mixed[:, n % 2], ident[:, :]).then_inc(s_pbl, 1)

            def group(i, g, last):
                gi = i * GPB + g
                xh, xl = xt_hi[:, g], xt_lo[:, g]
                pe.wait_ge(s_xlo, gi * GT + GT)
                for j in range(1 + NH):
                    if j >= 2:
                        pe.wait_ge(s_qk, gi * (1 + NH) + j - 1)
                    elif j == 0:
                        pe.wait_ge(s_st, gi * GT + 1)
                    three(B[j % 2], [(a_hi[:, k, j * D:(j + 1) * D], a_lo[:, k, j * D:(j + 1) * D],
                                      xh[:, k], xl[:, k]) for k in range(KC)], GRP).then_inc(s_pqk, 1)
                for t in range(GT):
                    cols = slice(t * P, (t + 1) * P)
                    if t >= 2:
                        pe.wait_ge(s_lg, gi * GT + t - 1)
                    elif t == 1:
                        pe.wait_ge(s_bl, gi * GT + FREE)
                    three(B[2 + t % 2], [(xh[:, k, cols], xl[:, k, cols], a_hi[:, k, CV:QKV], a_lo[:, k, CV:QKV])
                                         for k in range(KC)], HD + NH).then_inc(s_pv, 1)
                for m in range(FC):
                    M = FM[m]
                    if m >= 2:
                        pe.wait_ge(s_sg, gi * FC + m - 1)
                    else:
                        pe.wait_ge(s_g, gi * GT + FREE)
                    for off, bank, done in ((0, G[m % 2], s_pg), (W_UP, U[m % 2], s_pup)):
                        if off:
                            if m >= 2:
                                pe.wait_ge(s_h, gi * FC + m - 1)
                            else:
                                pe.wait_ge(s_y1, gi * GT + FREE)
                        w = [off + k * F + m * P for k in range(KC)]
                        three(bank, [(w_hi[:, c:c + M], w_lo[:, c:c + M], xh[:, k], xl[:, k])
                                     for k, c in enumerate(w)], GRP, M).then_inc(done, 1)
                    if m in SCORES:
                        scores(gi, g, m // 2, SCORES[m])
                    if m in BLEND:
                        blend(gi, m // 2 - 1)
                    if m in NEXT_T and not last:
                        pe.wait_ge(s_mix, (gi * GT + m // 2) * NMIX)
                        x_transposes(NEXT_T[m], gi * GT + GT + NEXT_T[m] + 1)
                    if m in RETRIEVE:
                        if m > 1:
                            if not last:
                                pe.wait_ge(s_xlo, gi * GT + GT + m // 2)
                            pe.wait_ge(s_bl, gi * GT + m // 2 + FREE)
                        else:
                            pe.wait_ge(s_lg, gi * GT + GT)
                        retrieve(i, g, m // 2, RETRIEVE[m])
                for t in range(GT):
                    cols = slice(t * P, (t + 1) * P)
                    bf, bs = G[(t + 1) % 2], U[(t + 1) % 2]
                    if t >= 2:
                        pe.wait_ge(s_g, gi * GT + t - 1 + FREE)
                    else:
                        pe.wait_ge(s_h, gi * FC + FC - 1 + t)
                    for k in range(FC):
                        K = FM[k]
                        if t == 0:
                            pe.wait_ge(s_hlo, gi * FC + k + 1)
                        c = W_DOWN + k * V
                        hh, hl = h_hi[0:K, k, cols], h_lo[0:K, k, cols]
                        wh, wl = w_hi[0:K, c:c + V], w_lo[0:K, c:c + V]
                        for n, (a, b) in enumerate(((hh, wh), (hh, wl), (hl, wh))):
                            ins = T_.matmul(bf[:, :], a, b, start=(k == 0 and n == 0), stop=(k == FC - 1 and n == 2))
                    ins.then_inc(s_pf, 1)
                    if t >= 2:
                        pe.wait_ge(s_y1, gi * GT + t - 1 + FREE)
                    if t == 0:
                        pe.wait_ge(s_bl, gi * GT + GT + FREE)
                    T_.matmul(bs[:, :], blend_t[:, t], wo_sb[:, :], start=True, stop=True).then_inc(s_pso, 1)

            pe.wait_ge(s_mrow, 16)
            T_.matmul(B[3][:, 0:HD], flip[:, :], mask_up.rearrange("p h t -> p (h t)"),
                      start=True, stop=True).then_inc(s_pmask, 1)
            pe.wait_ge(s_wst, 2 * NBLK)
            pe.wait_ge(s_alo, 4)
            pe.wait_ge(s_mask, 1)
            pe.wait_ge(s_wo, 16)
            with pe.Fori(0, NB - 1) as i:
                for g in range(GPB):
                    group(i, g, False)
            for g in range(GPB):
                group(NB - 1, g, g == GPB - 1)


def kernel(**inputs):
    import numpy as np
    import concourse.bacc as bacc
    from concourse.bass_utils import run_bass_kernel_spmd as run

    a = {k.replace("L0_", ""): np.ascontiguousarray(v) for k, v in inputs.items()}
    B, T, V = a["attn_x"].shape
    F = a["ffn_gate_idx"].shape[0]
    chunks = -(-F // 128)

    down = np.zeros((chunks * 128, V), a["ffn_down_idx"].dtype)
    down[:F] = a["ffn_down_idx"].T
    parts = [w.T.reshape(V // 128, 128, F).transpose(1, 0, 2).reshape(128, -1)
             for w in (a["ffn_gate_idx"], a["ffn_up_idx"])]
    parts.append(down.reshape(chunks, 128, V).transpose(1, 0, 2).reshape(128, -1))
    cols = sum(p.shape[1] for p in parts)
    blocks = -(-cols // 512)
    blocks += -blocks % 3
    idx = np.zeros((128, blocks * 512), down.dtype)
    idx[:, :cols] = np.concatenate(parts, 1)
    idx = idx.reshape(4, 32, blocks, 512).transpose(2, 1, 0, 3)

    arrays = {
        "x": a["attn_x"].reshape(B * T, V), "idx": idx, "lut": a["ffn_lut"],
        "wq": a["attn_Wq"], "wk": a["attn_Wk"], "wv": a["attn_Wv"], "wo": a["attn_Wo"], "wg": a["attn_Wg"],
        "decay_logits": a["attn_decay_logits"], "out_scale": a["attn_out_scale"].reshape(1),
    }
    arrays = {k: np.ascontiguousarray(v) for k, v in arrays.items()}
    nc = bacc.Bacc("TRN2", target_bir_lowering=False, num_devices=1)
    args = [nc.dram_tensor(f"in_{k}", v.shape, mybir.dt.from_np(v.dtype), kind="ExternalInput").ap()
            for k, v in arrays.items()]
    out = nc.dram_tensor("out_y", (B * T, V), F32, kind="ExternalOutput").ap()
    attention_ffn_kernel(nc, *args, out)
    r = run(nc, [{f"in_{k}": v for k, v in arrays.items()}], core_ids=[0])
    return r.results[0]["out_y"].reshape(B, T, V)
```

```python
from contextlib import ExitStack

import concourse.bass as bass
from concourse import mybir

ALU = mybir.AluOpType
ACT = mybir.ActivationFunctionType
AX = mybir.AxisListType
F32 = mybir.dt.float32
F16 = mybir.dt.float16
I32 = mybir.dt.int32
RADD = bass.bass_isa.ReduceOp.add

P = 128
BANK = 512
GT = 4
GRP = GT * P
NLUT = 16
CG = 4
QR = P // CG

XP = 10
WP = 8
FP = 14
TP = 14
QP = -14
SP = -16
HP = -(5 + 2 * WP + XP)

def attention_ffn_kernel(nc, x, idx, lut, wq, wk, wv, wo, wg, decay_logits, out_scale, out):
    NTOK, V = x.shape
    D = wq.shape[1]
    NH = wk.shape[0]
    KC = V // P
    F = 1376
    FC = -(-F // P)
    FM = [min(P, F - m * P) for m in range(FC)]
    T = 1024
    NB = NTOK // T
    GPB = T // GRP
    assert GPB == 2 and KC == 4 and D == P and V == BANK and NH == 3
    NBLK = idx.shape[0]
    HEAD = 3
    OP = [-QP, -QP, -QP - SP, XP]
    W_UP, W_DOWN = KC * F, 2 * KC * F
    UNR = 3
    assert NBLK % UNR == 0 and NBLK * BANK >= W_DOWN + FC * V
    QKV = (1 + 2 * NH) * D + NH
    CK, CV, CGT = D, (1 + NH) * D, (1 + 2 * NH) * D
    HD = NH * D
    VB = [2, 3, 0, 1]

    with ExitStack() as ctx:
        def sb(name, shape, dt):
            return ctx.enter_context(nc.sbuf_tensor(name, shape, dt))

        def ps(name, dt=F32):
            return ctx.enter_context(nc.psum_tensor(name, [P, BANK], dt))

        def sem(name):
            return ctx.enter_context(nc.semaphore(name))

        w_hi = sb("w_hi", [P, NBLK * BANK], F16)
        w_lo = sb("w_lo", [P, NBLK * BANK], F16)
        a_hi = sb("a_hi", [P, KC, QKV], F16)
        a_lo = sb("a_lo", [P, KC, QKV], F16)
        wo_hi = sb("wo_hi", [P, V], F16)
        wo_lo = sb("wo_lo", [P, V], F16)
        x_sb = sb("x_sb", [P, 2, GT, V], F32)
        xhat = sb("xhat", [P, GT, V], F32)
        xt_hi = sb("xt_hi", [P, 2, KC, GRP], F16)
        xt_lo = sb("xt_lo", [P, 2, KC, GRP], F16)
        n_qk, n_v = 2 * (1 + NH) * GRP // 2, 2 * GT * HD // 2
        attn = sb("attn", [P, n_qk + 2 * n_v], F32)

        def halves(lo, n, **dims):
            return attn[:, lo:lo + n].bitcast(F16).rearrange("p (s j c) -> p s j c", s=2, **dims)

        qk_hi, qk_lo = (halves(0, n_qk, j=1 + NH)[:, s] for s in range(2))
        v_hi, v_lo = (halves(n_qk, n_v, j=GT)[:, s] for s in range(2))
        vb_hi, vb_lo = (halves(n_qk + n_v, n_v, j=GT)[:, s] for s in range(2))
        q32 = sb("q32", [P, GRP], F32)
        state = sb("state", [P, HD], F32)
        faded = sb("faded", [P, HD], F32)
        mixed = sb("mixed", [P, D], F32)
        mixed_half = sb("mixed_half", [P, 2, 2, D], F16)
        ident = sb("ident", [P, P], F32)
        ident16 = sb("ident16", [P, P], F16)
        mask = sb("mask", [P, NH, P], F32)
        mask_up = faded[:, :].rearrange("p (h t) -> p h t", h=NH)
        fade_s = sb("fade_s", [P, NH], F32)
        flip = sb("flip", [P, P], F32)
        fade_end = sb("fade_end", [NH, P], F32)
        fade_rows = nc.dram_tensor("fade_rows", [NH, 2 * P], F32, kind="Internal")
        fade_t = sb("fade_t", [P, NH], F32)
        fade_tile = sb("fade_tile", [P, NH], F32)
        decay = sb("decay", [P, NH], F32)
        dlog = sb("dlog", [P, NH], F32)
        oscale = sb("oscale", [P, 1], F32)
        fade_q = sb("fade_q", [P, NH], F32)
        fade_v = sb("fade_v", [P, NH], F32)
        nhalf = sb("nhalf", [P, GT], F32)
        WO, LUT = 4, 5
        amax = sb("amax", [P, 6], F32)
        gsum = sb("gsum", [P, 5], F32)
        ebits = sb("ebits", [P, 6], I32)
        up_e = sb("up_e", [P, 6], I32)
        down_e = sb("down_e", [P, 6], I32)
        hf_e = sb("hf_e", [P, 2], I32)
        scale_up = sb("scale_up", [P, 6], I32)
        scale_down = sb("scale_down", [P, 6], I32)
        scale_hf = sb("scale_hf", [P, 2], I32)
        row_max = sb("row_max", [P, 1], F32)
        row_e = sb("row_e", [P, 1], I32)
        row_up = sb("row_up", [P, 1], I32)
        row_down = sb("row_down", [P, 1], I32)
        row_out = sb("row_out", [P, GT], F32)
        stats = sb("stats", [P, GT, 6], F32)
        moments = sb("moments", [P, GT, 2], F32)
        var = sb("var", [P, GT], F32)
        rstd = sb("rstd", [P, GT], F32)
        logit = sb("logit", [P, GT, NH], F32)
        lmax = sb("lmax", [P, GT], F32)
        lsub = sb("lsub", [P, GT, NH], F32)
        lth = sb("lth", [P, GT, NH], F32)
        lnum = sb("lnum", [P, GT, NH], F32)
        lden = sb("lden", [P, GT, NH], F32)
        lrec = sb("lrec", [P, GT, NH], F32)
        lexp = sb("lexp", [P, GT, NH], F32)
        lsum = sb("lsum", [P, GT], F32)
        lrs = sb("lrs", [P, GT], F32)
        gate = sb("gate", [P, GT, NH], F32)
        gate_t = sb("gate_t", [P, GT, NH], F32)
        lutrow = sb("lutrow", [P, NLUT], F32)
        lutcol = sb("lutcol", [P, CG], F32)
        lut_sc = sb("lut_sc", [P, CG], F32)
        lut_hi = sb("lut_hi", [P, CG], F16)
        lut_hi32 = sb("lut_hi32", [P, CG], F32)
        lut_lo32 = sb("lut_lo32", [P, CG], F32)
        pidx = sb("pidx", [P, 1], I32)
        pquad = sb("pquad", [P, 1], I32)
        code = sb("code", [P, CG], F32)
        eye4 = sb("eye4", [P, CG, QR], F32)
        eye = sb("eye", [P, QR], F32)
        pick_hi = sb("pick_hi", [P, CG, QR], F16)
        pick_lo = sb("pick_lo", [P, CG, QR], F16)

        HB = FC * GRP * 2
        sizes = dict(h_hi=HB, h_lo=HB, sg=2 * 2048, h32=2 * 2048, g=2 * 2048, y=GT * 2048,
                     bl=GRP * 4, kn=2 * HD * 4, pr=HD * 4, ph=2 * HD * 4, vb=HD * 4)
        build = UNR * CG * CG * BANK * 2
        region = sb("region", [P, max(sum(sizes.values()), build) // 4], F32)
        at = {}
        pos = 0
        for k, n in sizes.items():
            at[k] = region[:, pos // 4:(pos + n) // 4]
            pos += n
        h_hi = at["h_hi"].bitcast(F16).rearrange("p (m t) -> p m t", m=FC)
        h_lo = at["h_lo"].bitcast(F16).rearrange("p (m t) -> p m t", m=FC)
        sg = at["sg"].rearrange("p (b t) -> p b t", b=2)
        h32 = at["h32"].rearrange("p (b t) -> p b t", b=2)
        g_sb = at["g"].rearrange("p (b t) -> p b t", b=2)
        y_sb = at["y"].rearrange("p (b t) -> p b t", b=GT)
        blend_t = at["bl"].bitcast(F16).rearrange("p (b s t) -> p b s t", b=GT, s=2)
        k_nat = at["kn"].bitcast(F16).rearrange("p (b s t) -> p b s t", b=2, s=2)
        probs = at["pr"]
        pr_half = at["ph"].bitcast(F16).rearrange("p (b s t) -> p b s t", b=2, s=2)
        vb32 = at["vb"]
        n_oh = UNR * CG * CG * BANK // 2
        onehot = region[:, 0:n_oh].bitcast(F16).rearrange("p (u j q c) -> p u j q c", u=UNR, j=CG, q=CG)
        wo32 = q32
        a32 = attn[:, 0:KC * QKV].rearrange("p (k c) -> p k c", k=KC)
        n_ix = CG * BANK // 2
        spare = x_sb[:, 1].rearrange("p t v -> p (t v)")
        codes = [c.bitcast(F16).rearrange("p (q c) -> p q c", q=CG)
                 for c in (attn[:, KC * QKV:KC * QKV + n_ix], spare[:, 0:n_ix], spare[:, n_ix:2 * n_ix])]

        G = [ps("G0"), ps("G1")]
        U = [ps("U0"), ps("U1")]
        B = [ps("B0"), ps("B1"), ps("B2"), ps("B3")]
        LUHI = [G[0], G[1], B[0]]
        LULO = [U[0], U[1], B[1]]

        s_x = [sem("x_in0"), sem("x_in1")]
        s_y = [sem(f"y_out{t}") for t in range(GT)]
        s_idx = [sem(f"codes_in{u}") for u in range(UNR)]
        s_w = sem("qkv_in")
        s_wo = sem("wo_in")
        s_small = sem("small_in")
        s_const = sem("const_ready")
        s_cstep = sem("const_step")
        s_init = sem("init_step")
        s_sq = sem("squares_ready")
        s_gsum = sem("norms_ready")
        s_lscale = sem("lut_scales_ready")
        s_osc = sem("out_scale_step")
        s_id16 = sem("ident16_ready")
        s_scale = sem("scales_ready")
        s_dec = sem("decay_step")
        s_pow = sem("power_step")
        s_pick = sem("pick_ready")
        s_row = sem("fade_rows_written")
        s_mrow = sem("mask_rows_in")
        s_pmask = sem("mask_in_psum")
        s_mask = sem("mask_ready")
        s_lhi = sem("lut_step")
        s_ahi = sem("a_hi_ready")
        s_alo = sem("a_lo_ready")
        s_oh = sem("onehot_ready")
        s_lu = sem("lookup_done")
        s_wst = sem("w_stored")
        s_bn = sem("bn_done")
        s_mv = sem("moments_done")
        s_var = sem("var_done")
        s_rstd = sem("rstd_done")
        s_xh = sem("xhat_ready")
        s_xt = sem("xt_in_psum")
        s_xhi = sem("xt_hi_ready")
        s_xlo = sem("xt_lo_ready")
        s_pqk = sem("qk_in_psum")
        s_q32 = sem("q_ready")
        s_qk = sem("qk_hi_ready")
        s_qkl = sem("qk_lo_ready")
        s_pv = sem("v_in_psum")
        s_v = sem("v_hi_ready")
        s_vl = sem("v_lo_ready")
        s_lg = sem("logits_ready")
        s_vb = sem("vb_ready")
        s_vbh = sem("vb_hi_ready")
        s_vbl = sem("vb_lo_ready")
        s_sm = sem("softmax_step")
        s_th = sem("tanh_ready")
        s_pkn = sem("k_nat_in_psum")
        s_kn = sem("k_nat_ready")
        s_psc = sem("scores_in_psum")
        s_pr = sem("probs_ready")
        s_prh = sem("probs_hi_ready")
        s_prl = sem("probs_lo_ready")
        s_pat = sem("retrieved_in_psum")
        s_mix = sem("mix_step")
        s_rs = sem("row_scale_step")
        s_pu = sem("update_in_psum")
        s_fade = sem("state_faded")
        s_st = sem("state_ready")
        s_pbl = sem("blend_in_psum")
        s_bl = sem("blend_ready")
        s_pg = sem("gate_in_psum")
        s_pup = sem("up_in_psum")
        s_sg = sem("silu_ready")
        s_h = sem("h_ready")
        s_hhi = sem("h_hi_ready")
        s_hlo = sem("h_lo_ready")
        s_pf = sem("ffn_in_psum")
        s_pso = sem("attn_in_psum")
        s_g = sem("g_ready")
        s_y1 = sem("product_ready")
        s_yr = sem("y_ready")

        x_v = x.rearrange("(n t p) v -> n p t v", t=GT, p=P)
        out_v = out.rearrange("(n t p) v -> n p t v", t=GT, p=P)

        f_up = scale_up[:, :].bitcast(F32)
        f_down = scale_down[:, :].bitcast(F32)
        f_hf = scale_hf[:, :].bitcast(F32)

        SCORES = {0: 3, 2: 2, 4: 1, 6: 0}
        RETRIEVE = {1: 3, 3: 2, 5: 1, 7: 0}
        BLEND = {2: 3, 4: 2, 6: 1, 8: 0}
        NEXT_T = {2: 0, 4: 1, 6: 2, 8: 3}
        PARTS = ((0, CK), (CK, CV), (CV, CGT), (CGT, QKV))
        NSM = 10
        NMIX = 2 * NH
        NRS = 8
        LOWS = [(n, k) for n in range(len(PARTS)) for k in range(KC)] + [(WO, 0)]

        FREE = 1

        def row_group(i, g):
            return i * GPB + (GPB - 1 - g)

        block = ctx.enter_context(nc.Block())

        @block.sync
        def _(sp):
            for t in range(GT):
                sp.sem_inc(s_y[t], 16 * FREE)
            sp.dma_start(lutrow[:, :], lut.partition_broadcast(P)).then_inc(s_small, 16)
            for c in range(CG):
                src = lut.rearrange("(j c) -> c j", c=CG)[c]
                sp.dma_start(lutcol[QR * c:QR * (c + 1), :], src.partition_broadcast(QR),
                             allow_slow_non_contiguous=True).then_inc(s_small, 16)
            sp.dma_start(dlog[:, :], decay_logits.partition_broadcast(P)).then_inc(s_small, 16)
            sp.dma_start(oscale[:, :], out_scale.partition_broadcast(P)).then_inc(s_small, 16)
            sp.dma_start(x_sb[:, 0], x_v[row_group(0, 0)]).then_inc(s_x[0], 16)
            sp.dma_start(a32[:, :, 0:D], wq.rearrange("(c p) d -> p c d", p=P)).then_inc(s_w, 16)
            for h in range(NH):
                sp.dma_start(a32[:, :, CK + h * D:CK + (h + 1) * D],
                             wk[h].rearrange("(c p) d -> p c d", p=P)).then_inc(s_w, 16)
                sp.dma_start(a32[:, :, CV + h * D:CV + (h + 1) * D],
                             wv[h].rearrange("(c p) d -> p c d", p=P)).then_inc(s_w, 16)
            sp.dma_start(a32[:, :, CGT:QKV], wg.rearrange("(c p) d -> p c d", p=P)).then_inc(s_w, 16)
            sp.dma_start(wo32[:, :], wo).then_inc(s_wo, 16)

            with nc.allow_non_contiguous_dma(reason="384 values, once"):
                sp.wait_ge(s_cstep, 5)
                sp.dma_start(fade_rows[:, P:2 * P], fade_end[:, :]).then_inc(s_row, 16)
                sp.wait_ge(s_pow, 1)
                sp.dma_start(fade_rows[:, 0:P].rearrange("h t -> t h"), fade_t[:, :]).then_inc(s_row, 16)
                sp.wait_ge(s_row, 32)
                sp.dma_start(mask_up[:, :, :], bass.AP(fade_rows, 1, [[1, P], [2 * P, NH], [1, P]])).then_inc(s_mrow, 16)
            sp.wait_ge(s_oh, CG * NBLK)

            def group(i, g, last):
                gi = i * GPB + g
                if not last:
                    sp.wait_ge(s_yr, gi * GT + FREE)
                    nxt = row_group(i + (g + 1) // GPB, (g + 1) % GPB)
                    sp.dma_start(x_sb[:, 1 - g], x_v[nxt]).then_inc(s_x[1 - g], 16)
                for t in range(GT):
                    sp.wait_ge(s_yr, gi * GT + t + 1 + FREE)
                    sp.dma_start(out_v[row_group(i, g)][:, t], y_sb[:, t]).then_inc(s_y[t], 16)

            with sp.Fori(0, NB - 1) as i:
                for g in range(GPB):
                    group(i, g, False)
            for g in range(GPB):
                group(NB - 1, g, g == GPB - 1)
            for t in range(GT):
                sp.wait_ge(s_y[t], 16 * (NB * GPB + FREE))

        @block.gpsimd
        def _(pool):
            def load_codes(b):
                u = b % UNR
                if b >= UNR:
                    pool.wait_ge(s_oh, CG * (b - UNR + 1))
                rows = idx[b].rearrange("p q c -> p (q c)").unsqueeze(0).broadcast_to([CG, QR, CG * BANK])
                pool.dma_start(codes[u].rearrange("p q c -> p (q c)"), rows).then_inc(s_idx[u], 16)

            for b in range(UNR):
                load_codes(b)
            nc.gpsimd.iota(pidx[:, :], pattern=[[0, 1]], base=0, channel_multiplier=1).then_inc(s_const, 1)
            nc.gpsimd.memset(eye4[:, :, :], 0.0).then_inc(s_cstep, 1)
            nc.gpsimd.memset(ident[:, :], 0.0).then_inc(s_cstep, 1)
            nc.gpsimd.memset(flip[:, :], 0.0).then_inc(s_cstep, 1)
            nc.gpsimd.memset(nhalf[:, :], -0.5).then_inc(s_cstep, 1)
            nc.gpsimd.memset(fade_end[:, :], 0.0).then_inc(s_cstep, 1)
            pool.wait_ge(s_cstep, 5)
            nc.gpsimd.affine_select(out=eye4[:, :, :], in_=eye4[:, :, :], compare_op=ALU.not_equal, fill=1.0, base=0,
                                    pattern=[[-QR, CG], [-1, QR]], channel_multiplier=1).then_inc(s_const, 1)
            nc.gpsimd.affine_select(out=ident[:, :], in_=ident[:, :], compare_op=ALU.not_equal, fill=1.0, base=0,
                                    pattern=[[-1, P]], channel_multiplier=1).then_inc(s_const, 1)
            nc.gpsimd.affine_select(out=flip[:, :], in_=flip[:, :], compare_op=ALU.not_equal, fill=1.0,
                                    base=-(P - 1), pattern=[[1, P]], channel_multiplier=1).then_inc(s_const, 1)
            for b in range(UNR, 2 * UNR - 1):
                load_codes(b)
            pool.wait_ge(s_var, 2)
            nc.gpsimd.tensor_tensor(rstd[:, :], var[:, :], nhalf[:, :], ALU.pow).then_inc(s_rstd, 1)
            load_codes(2 * UNR - 1)
            nc.gpsimd.iota(fade_s[:, :], pattern=[[0, NH]], base=0, channel_multiplier=1,
                           allow_small_or_imprecise_dtypes=True).then_inc(s_cstep, 1)
            nc.gpsimd.iota(fade_t[:, :], pattern=[[0, NH]], base=P - 1, channel_multiplier=-1,
                           allow_small_or_imprecise_dtypes=True).then_inc(s_cstep, 1)
            nc.gpsimd.memset(fade_tile[:, :], float(P)).then_inc(s_cstep, 1)
            pool.wait_ge(s_dec, 3)
            pool.wait_ge(s_cstep, 8)
            for m in (fade_t, fade_s, fade_tile):
                nc.gpsimd.tensor_tensor(m[:, :], decay[:, :], m[:, :], ALU.pow).then_inc(s_pow, 1)
            for b in range(2 * UNR, 3 * UNR):
                load_codes(b)
            pool.wait_ge(s_sq, 5)
            nc.gpsimd.partition_all_reduce(gsum[:, :], amax[:, 0:5], P, RADD).then_inc(s_gsum, 1)
            def a_low(n, k):
                pool.wait_ge(s_ahi, 2 * n + 2)
                if n == WO:
                    dst, src, high = wo_lo[:, :], wo32[:, :], wo_hi[:, :]
                else:
                    a, b = PARTS[n]
                    dst, src, high = a_lo[:, k, a:b], a32[:, k, a:b], a_hi[:, k, a:b]
                nc.gpsimd.tensor_tensor(dst, src, high, ALU.subtract).then_inc(s_alo, 1)

            lows = list(LOWS)
            for b in range(3 * UNR, NBLK):
                load_codes(b)
                if b >= 4 * UNR and lows:
                    a_low(*lows.pop(0))
            for n, k in lows:
                a_low(n, k)
            def group(i, g):
                gi = i * GPB + g
                pool.wait_ge(s_var, 2 * gi + 4)
                nc.gpsimd.tensor_tensor(rstd[:, :], var[:, :], nhalf[:, :], ALU.pow).then_inc(s_rstd, 1)

            with pool.Fori(0, NB - 1) as i:
                for g in range(GPB):
                    group(i, g)
            group(NB - 1, 0)

        @block.scalar
        def _(act):
            act.sem_inc(s_g, FREE)
            act.sem_inc(s_bl, FREE)
            act.wait_ge(s_small, 16 * (CG + 3))
            nc.scalar.activation(decay[:, :], dlog[:, :], ACT.Exp, scale=-1.0).then_inc(s_dec, 1)

            def xt_high(par, t, n):
                act.wait_ge(s_xt, n)
                nc.scalar.activation(xt_hi[:, par, :, t * P:(t + 1) * P],
                                     B[2][:, :].rearrange("p (k c) -> p k c", k=KC), ACT.Copy).then_inc(s_xhi, 1)

            act.wait_ge(s_w, 16 * (2 + 2 * NH))
            for n, (a, b) in enumerate(PARTS):
                nc.scalar.activation(a_hi[:, :, a:b], a32[:, :, a:b], ACT.Square,
                                     accum_out=amax[:, n:n + 1]).then_inc(s_sq, 1)
            act.wait_ge(s_wo, 16)
            nc.scalar.activation(wo_hi[:, :], wo32[:, :], ACT.Square, accum_out=amax[:, WO:WO + 1]).then_inc(s_sq, 1)

            def a_high():
                act.wait_ge(s_scale, 2)
                for n, (a, b) in enumerate(PARTS):
                    nc.scalar.activation(a32[:, :, a:b], a32[:, :, a:b], ACT.Copy,
                                         scale=f_up[:, n:n + 1]).then_inc(s_ahi, 1)
                    act.wait_ge(s_ahi, 2 * n + 1)
                    nc.scalar.activation(a_hi[:, :, a:b], a32[:, :, a:b], ACT.Copy).then_inc(s_ahi, 1)
                nc.scalar.activation(wo32[:, :], wo32[:, :], ACT.Copy, scale=f_up[:, WO:WO + 1]).then_inc(s_ahi, 1)
                act.wait_ge(s_ahi, 2 * WO + 1)
                nc.scalar.activation(wo_hi[:, :], wo32[:, :], ACT.Copy).then_inc(s_ahi, 1)

            def store(i, u):
                b = i * UNR + u
                col = bass.ds(b * BANK, BANK)
                act.wait_ge(s_lu, b + 1)
                nc.scalar.activation(w_hi[:, col], LUHI[u][:, :], ACT.Copy).then_inc(s_wst, 1)
                nc.scalar.activation(w_lo[:, col], LULO[u][:, :], ACT.Copy).then_inc(s_wst, 1)

            for i in range(HEAD):
                for u in range(UNR):
                    store(i, u)
                    if 0 <= (i - 1) * UNR + u < GT:
                        t = (i - 1) * UNR + u
                        xt_high(0, t, t + 1)
            a_high()
            with act.Fori(HEAD, NBLK // UNR) as i:
                for u in range(UNR):
                    store(i, u)
            act.wait_ge(s_pmask, 1)
            nc.scalar.activation(mask[:, :, :].rearrange("p h t -> p (h t)"), B[3][:, 0:HD], ACT.Copy,
                                 scale=2.0 ** SP).then_inc(s_mask, 1)

            def group(i, g, last):
                gi = i * GPB + g
                for j in range(1 + NH):
                    act.wait_ge(s_pqk, gi * (1 + NH) + j + 1)
                    if j == 0:
                        nc.scalar.activation(q32[:, :], B[0][:, :], ACT.Copy, scale=2.0 ** QP).then_inc(s_q32, 1)
                    nc.scalar.activation(qk_hi[:, j], B[j % 2][:, :], ACT.Copy, scale=2.0 ** QP).then_inc(s_qk, 1)
                for t in range(GT):
                    act.wait_ge(s_pv, gi * GT + t + 1)
                    nc.scalar.activation(v_hi[:, t], B[VB[t]][:, 0:HD], ACT.Copy, scale=2.0 ** QP).then_inc(s_v, 1)
                    nc.scalar.activation(logit[:, t], B[VB[t]][:, HD:HD + NH], ACT.Copy,
                                         scale=f_down[:, 3:4]).then_inc(s_lg, 1)
                    act.wait_ge(s_vb, gi * GT + t + 1)
                    nc.scalar.activation(vb_hi[:, t], vb32[:, :], ACT.Copy).then_inc(s_vbh, 1)
                act.wait_ge(s_sm, gi * NSM + 2)
                nc.scalar.activation(lth[:, :, :], lsub[:, :, :], ACT.Tanh, scale=0.5).then_inc(s_th, 1)
                for m in range(FC):
                    M = FM[m]
                    act.wait_ge(s_pg, gi * FC + m + 1)
                    if m >= 2:
                        act.wait_ge(s_h, gi * FC + m - 1)
                    nc.scalar.activation(sg[0:M, m % 2], G[m % 2][0:M, :], ACT.Silu,
                                         scale=f_down[0:M, LUT:LUT + 1]).then_inc(s_sg, 1)
                    act.wait_ge(s_h, gi * FC + m + 1)
                    nc.scalar.activation(h_hi[0:M, m], h32[0:M, m % 2], ACT.Copy).then_inc(s_hhi, 1)
                    if m in SCORES:
                        n = m // 2
                        act.wait_ge(s_pkn, gi * GT + n + 1)
                        nc.scalar.activation(k_nat[:, n % 2].rearrange("p s t -> p (s t)"),
                                             B[0][:, :].bitcast(F16)[:, 0:2 * HD], ACT.Copy).then_inc(s_kn, 1)
                        act.wait_ge(s_pr, gi * GT + n + 1)
                        nc.scalar.activation(pr_half[:, n % 2, 0], probs[:, :], ACT.Copy).then_inc(s_prh, 1)
                    if m in NEXT_T and not last:
                        xt_high(1 - g, NEXT_T[m], gi * GT + GT + NEXT_T[m] + 1)
                    if m in BLEND:
                        act.wait_ge(s_pbl, gi * GT + m // 2)
                        nc.scalar.activation(blend_t[:, BLEND[m]].rearrange("p s t -> p (s t)"),
                                             B[3][:, :].bitcast(F16)[:, 0:2 * P], ACT.Copy).then_inc(s_bl, 1)
                for t in range(GT):
                    act.wait_ge(s_pf, gi * GT + t + 1)
                    if t >= 2:
                        act.wait_ge(s_y1, gi * GT + t - 1 + FREE)
                    nc.scalar.activation(g_sb[:, t % 2], G[(t + 1) % 2][:, :], ACT.Silu,
                                         scale=f_hf[:, 1:2]).then_inc(s_g, 1)

            with act.Fori(0, NB - 1) as i:
                for g in range(GPB):
                    group(i, g, False)
            for g in range(GPB):
                group(NB - 1, g, g == GPB - 1)

        @block.vector
        def _(dve):
            V_ = nc.vector
            dve.sem_inc(s_y1, FREE)
            dve.sem_inc(s_yr, FREE)
            init = [0]

            def step(ins):
                init[0] += 1
                ins.then_inc(s_init, 1)
                dve.wait_ge(s_init, init[0])

            def norm(par, loads, gi, t0=0):
                def aggregate(t):
                    V_.bn_aggr(moments[:, t], stats[:, t]).then_inc(s_mv, 1)

                def variance(a, b):
                    V_.tensor_scalar(var[:, a:b], moments[:, a:b, 1], 1e-5, 2.0 ** (-2 * XP), ALU.add,
                                     ALU.mult).then_inc(s_var, 1)

                n0 = gi * GT
                dve.wait_ge(s_x[par], loads)
                for t in range(GT):
                    if t >= 2:
                        dve.wait_ge(s_bn, n0 + t - 1)
                    V_.bn_stats(stats[:, t], x_sb[:, par, t]).then_inc(s_bn, 1)
                    if t >= 2:
                        aggregate(t - 2)
                dve.wait_ge(s_bn, n0 + GT)
                dve.wait_ge(s_mv, n0 + 2)
                variance(0, 2)
                aggregate(2)
                aggregate(3)
                dve.wait_ge(s_mv, n0 + GT)
                variance(2, 4)

            def xhat_tile(par, gi, t):
                if t == 0:
                    dve.wait_ge(s_rstd, gi + 1)
                V_.tensor_scalar(xhat[:, t], x_sb[:, par, t], moments[:, t, 0:1], rstd[:, t:t + 1],
                                 ALU.subtract, ALU.mult).then_inc(s_xh, 1)

            def xt_low(par, t, n):
                dve.wait_ge(s_xhi, n)
                V_.tensor_tensor(xt_lo[:, par, :, t * P:(t + 1) * P],
                                 B[2][:, :].rearrange("p (k c) -> p k c", k=KC),
                                 xt_hi[:, par, :, t * P:(t + 1) * P], ALU.subtract).then_inc(s_xlo, 1)

            def compare(i, u, first):
                b = i * UNR + u
                dve.wait_ge(s_idx[u], 16 * i + 16)
                if not first:
                    dve.wait_ge(s_lu, b - UNR + 1)
                for j in range(CG):
                    V_.tensor_scalar(onehot[:, u, j], codes[u], code[:, j:j + 1], None,
                                     ALU.is_equal).then_inc(s_oh, 1)

            dve.wait_ge(s_const, 1)
            step(V_.tensor_scalar(pquad[:, :], pidx[:, :], 5, None, ALU.logical_shift_right))
            for j in range(CG):
                ins = V_.tensor_scalar(code[:, j:j + 1], pquad[:, :], float(CG * j), None, ALU.add)
                ins.then_inc(s_init, 1)
                init[0] += 1
            dve.wait_ge(s_init, init[0])

            def exponents(src, cols, lo, hi):
                step(V_.tensor_scalar(ebits[:, cols], src.bitcast(I32), 23, None, ALU.logical_shift_right))
                if cols.start == 0:
                    step(V_.tensor_scalar(ebits[:, cols], ebits[:, cols], 127, None, ALU.add))
                    step(V_.tensor_scalar(ebits[:, cols], ebits[:, cols], 1, None, ALU.logical_shift_right))
                step(V_.tensor_scalar(ebits[:, cols], ebits[:, cols], lo, hi, ALU.max, ALU.min))
                up = FP if cols.start == 0 else WP
                step(V_.tensor_scalar(up_e[:, cols], ebits[:, cols], -1.0, 254.0 + up, ALU.mult, ALU.add))
                step(V_.tensor_scalar(down_e[:, cols], ebits[:, cols], float(-up - XP), None, ALU.add))

            def shifted(dst, src, done):
                V_.tensor_scalar(dst, src, 23, None, ALU.logical_shift_left).then_inc(done, 1)

            dve.wait_ge(s_small, 16 * (CG + 3))
            step(V_.tensor_reduce(amax[:, LUT:LUT + 1], lutrow[:, :], AX.X, ALU.max, apply_absolute_value=True))
            exponents(amax[:, LUT:LUT + 1], slice(LUT, LUT + 1), 90.0, 165.0)
            step(V_.tensor_scalar(hf_e[:, 0:1], ebits[:, LUT:LUT + 1], -1.0, 254.0 + WP + HP, ALU.mult, ALU.add))
            step(V_.tensor_scalar(hf_e[:, 1:2], ebits[:, LUT:LUT + 1], 3.0, 127.0 - 3 * 127 - 3 * WP - XP - HP,
                                  ALU.mult, ALU.add))
            shifted(scale_up[:, LUT:LUT + 1], up_e[:, LUT:LUT + 1], s_lscale)
            shifted(scale_down[:, LUT:LUT + 1], down_e[:, LUT:LUT + 1], s_lscale)
            shifted(scale_hf[:, :], hf_e[:, :], s_lscale)
            dve.wait_ge(s_lscale, 3)

            step(V_.tensor_scalar(lut_sc[:, :], lutcol[:, :], f_up[:, LUT:LUT + 1], None, ALU.mult))
            step(V_.tensor_copy(lut_hi[:, :], lut_sc[:, :]))
            step(V_.tensor_copy(lut_hi32[:, :], lut_hi[:, :]))
            step(V_.tensor_tensor(lut_lo32[:, :], lut_sc[:, :], lut_hi32[:, :], ALU.subtract))
            dve.wait_ge(s_const, 4)
            step(V_.tensor_reduce(eye[:, :], eye4[:, :, :].rearrange("p a c -> p c a"), AX.X, ALU.add))
            for j in range(CG):
                V_.tensor_scalar(pick_hi[:, j], eye[:, :], lut_hi32[:, j:j + 1], None, ALU.mult).then_inc(s_pick, 1)
                V_.tensor_scalar(pick_lo[:, j], eye[:, :], lut_lo32[:, j:j + 1], None, ALU.mult).then_inc(s_pick, 1)

            for i in range(HEAD):
                for u in range(UNR):
                    compare(i, u, i == 0)
                    if i == 0 and u == 0:
                        V_.tensor_copy(ident16[:, :], ident[:, :]).then_inc(s_id16, 1)
                        dve.wait_ge(s_dec, 1)
                        V_.tensor_scalar(decay[:, :], decay[:, :], 1.0, None, ALU.add).then_inc(s_dec, 1)
                        dve.wait_ge(s_dec, 2)
                        V_.reciprocal(decay[:, :], decay[:, :]).then_inc(s_dec, 1)
                    if i == 0 and u == 1:
                        norm(0, 16, 0)
                    if i == 1 and u == 0:
                        for t in range(GT):
                            xhat_tile(0, 0, t)
                    if 0 <= (i - 1) * UNR + u - 1 < GT:
                        t = (i - 1) * UNR + u - 1
                        xt_low(0, t, t + 1)
            dve.wait_ge(s_gsum, 1)
            exponents(gsum[:, :], slice(0, LUT), 40.0, 200.0)
            shifted(scale_up[:, 0:LUT], up_e[:, 0:LUT], s_scale)
            shifted(scale_down[:, 0:LUT], down_e[:, 0:LUT], s_scale)

            with dve.Fori(HEAD, NBLK // UNR) as i:
                for u in range(UNR):
                    compare(i, u, False)

            V_.memset(state[:, :], 0.0).then_inc(s_st, 1)
            for m, n in enumerate((0, 1, 2, WO)):
                V_.tensor_scalar(oscale[:, :], oscale[:, :], f_down[:, n:n + 1], 2.0 ** OP[m], ALU.mult,
                                 ALU.mult).then_inc(s_osc, 1)
                dve.wait_ge(s_osc, m + 1)
            dve.wait_ge(s_pow, 3)
            V_.tensor_scalar(fade_q[:, :], fade_t[:, :], 2.0 ** SP, None, ALU.mult).then_inc(s_osc, 1)
            V_.tensor_scalar(fade_v[:, :], fade_s[:, :], 2.0 ** QP, None, ALU.mult).then_inc(s_osc, 1)
            dve.wait_ge(s_osc, 6)

            def heads(ap):
                return ap.rearrange("p (h c) -> p h c", h=NH)

            def spread(col):
                return col[:, :].unsqueeze(2).broadcast_to([P, NH, P])

            def softmax(gi):
                n0 = gi * NSM
                wide = lambda ap: ap[:, :].unsqueeze(2).broadcast_to([P, GT, NH])
                dve.wait_ge(s_lg, gi * GT + GT)
                V_.tensor_reduce(lmax[:, :], logit[:, :, :], AX.X, ALU.max).then_inc(s_sm, 1)
                dve.wait_ge(s_sm, n0 + 1)
                V_.tensor_tensor(lsub[:, :, :], logit[:, :, :], wide(lmax), ALU.subtract).then_inc(s_sm, 1)
                dve.wait_ge(s_th, gi + 1)
                V_.tensor_scalar(lnum[:, :, :], lth[:, :, :], 1.0, None, ALU.add).then_inc(s_sm, 1)
                V_.tensor_scalar(lden[:, :, :], lth[:, :, :], -1.0, 1.0, ALU.mult, ALU.add).then_inc(s_sm, 1)
                dve.wait_ge(s_sm, n0 + 4)
                V_.reciprocal(lrec[:, :, :], lden[:, :, :]).then_inc(s_sm, 1)
                dve.wait_ge(s_sm, n0 + 5)
                V_.tensor_tensor(lexp[:, :, :], lnum[:, :, :], lrec[:, :, :], ALU.mult).then_inc(s_sm, 1)
                dve.wait_ge(s_sm, n0 + 6)
                V_.tensor_reduce(lsum[:, :], lexp[:, :, :], AX.X, ALU.add).then_inc(s_sm, 1)
                dve.wait_ge(s_sm, n0 + 7)
                V_.reciprocal(lrs[:, :], lsum[:, :]).then_inc(s_sm, 1)
                dve.wait_ge(s_sm, n0 + 8)
                V_.tensor_tensor(gate[:, :, :], lexp[:, :, :], wide(lrs), ALU.mult).then_inc(s_sm, 1)
                dve.wait_ge(s_sm, n0 + 9)
                V_.tensor_tensor(gate_t[:, :, :], gate[:, :, :],
                                 fade_q[:, :].unsqueeze(1).broadcast_to([P, GT, NH]), ALU.mult).then_inc(s_sm, 1)

            def mix(gi, g, n, t):
                c0 = (gi * GT + n) * NMIX
                dve.wait_ge(s_pat, gi * GT + n + 1)
                if n == 0:
                    dve.wait_ge(s_sm, gi * NSM + NSM)
                else:
                    dve.wait_ge(s_rs, (gi * GT + n) * NRS)
                acc = mixed[:, :]
                V_.tensor_scalar(acc, B[3][:, 0:D], gate[:, t, 0:1], None, ALU.mult).then_inc(s_mix, 1)
                for h in range(1, NH):
                    dve.wait_ge(s_mix, c0 + h)
                    V_.scalar_tensor_tensor(out=acc, in0=B[3][:, h * D:(h + 1) * D], scalar=gate[:, t, h:h + 1],
                                            in1=acc, op0=ALU.mult, op1=ALU.add).then_inc(s_mix, 1)
                for h in range(NH):
                    dve.wait_ge(s_mix, c0 + NH + h)
                    V_.scalar_tensor_tensor(out=acc, in0=B[2][:, h * D:(h + 1) * D], scalar=gate_t[:, t, h:h + 1],
                                            in1=acc, op0=ALU.mult, op1=ALU.add).then_inc(s_mix, 1)

            def split_rows(gi, n, t):
                c0 = (gi * GT + n) * NRS
                dve.wait_ge(s_mix, (gi * GT + n + 1) * NMIX)
                V_.tensor_reduce(row_max[:, :], mixed[:, :], AX.X, ALU.max, apply_absolute_value=True).then_inc(s_rs, 1)
                dve.wait_ge(s_rs, c0 + 1)
                V_.tensor_scalar(row_e[:, :], row_max[:, :].bitcast(I32), 23, None,
                                 ALU.logical_shift_right).then_inc(s_rs, 1)
                dve.wait_ge(s_rs, c0 + 2)
                V_.tensor_scalar(row_e[:, :], row_e[:, :], 30.0, 230.0, ALU.max, ALU.min).then_inc(s_rs, 1)
                dve.wait_ge(s_rs, c0 + 3)
                V_.tensor_scalar(row_up[:, :], row_e[:, :], -2.0 ** 23, (254.0 + TP) * 2.0 ** 23, ALU.mult,
                                 ALU.add).then_inc(s_rs, 1)
                V_.tensor_scalar(row_down[:, :], row_e[:, :], 2.0 ** 23, -TP * 2.0 ** 23, ALU.mult,
                                 ALU.add).then_inc(s_rs, 1)
                dve.wait_ge(s_rs, c0 + 5)
                up = row_up[:, :].bitcast(F32)
                V_.tensor_scalar(mixed_half[:, n % 2, 0], mixed[:, :], up, None, ALU.mult).then_inc(s_rs, 1)
                V_.tensor_scalar(row_out[:, t:t + 1], row_down[:, :].bitcast(F32), oscale[:, 0:1], None,
                                 ALU.mult).then_inc(s_rs, 1)
                dve.wait_ge(s_rs, c0 + 7)
                V_.scalar_tensor_tensor(out=mixed_half[:, n % 2, 1], in0=mixed[:, :], scalar=up,
                                        in1=mixed_half[:, n % 2, 0], op0=ALU.mult, op1=ALU.subtract).then_inc(s_rs, 1)

            def update_state(i, g, n):
                if n == GT - 1 and g == GPB - 1:
                    dve.wait_ge(s_pat, (i * GPB + g) * GT + n + 1)
                    V_.memset(state[:, :], 0.0).then_inc(s_st, 1)
                    return
                k = i * (GPB * GT - 1) + g * GT + n
                dve.wait_ge(s_st, i * GPB * GT + g * GT + n + 1)
                V_.tensor_tensor(heads(faded[:, :]), heads(state[:, :]), spread(fade_tile), ALU.mult).then_inc(s_fade, 1)
                dve.wait_ge(s_fade, k + 1)
                dve.wait_ge(s_pu, k + 1)
                V_.tensor_tensor(state[:, :], B[0][:, 0:HD], faded[:, :], ALU.add).then_inc(s_st, 1)

            def group(i, g, last):
                gi = i * GPB + g
                for j in range(1 + NH):
                    if j == 0:
                        dve.wait_ge(s_q32, gi + 1)
                    dve.wait_ge(s_qk, gi * (1 + NH) + j + 1)
                    V_.scalar_tensor_tensor(out=qk_lo[:, j], in0=B[j % 2][:, :], scalar=2.0 ** QP, in1=qk_hi[:, j],
                                            op0=ALU.mult, op1=ALU.subtract).then_inc(s_qkl, 1)
                if not last:
                    norm(1 - g, 16 * (i + g) + 16, gi + 1)
                for t in range(GT):
                    dve.wait_ge(s_lg, gi * GT + t + 1)
                    if t:
                        dve.wait_ge(s_vbl, gi * GT + t)
                    V_.tensor_tensor(heads(vb32[:, :]), heads(B[VB[t]][:, 0:HD]), spread(fade_v),
                                     ALU.mult).then_inc(s_vb, 1)
                    V_.scalar_tensor_tensor(out=v_lo[:, t], in0=B[VB[t]][:, 0:HD], scalar=2.0 ** QP, in1=v_hi[:, t],
                                            op0=ALU.mult, op1=ALU.subtract).then_inc(s_vl, 1)
                    dve.wait_ge(s_vbh, gi * GT + t + 1)
                    V_.tensor_tensor(vb_lo[:, t], vb32[:, :], vb_hi[:, t], ALU.subtract).then_inc(s_vbl, 1)
                softmax(gi)
                if not last:
                    for t in range(GT):
                        xhat_tile(1 - g, gi + 1, t)

                def low(m):
                    M = FM[m]
                    dve.wait_ge(s_hhi, gi * FC + m + 1)
                    V_.tensor_tensor(h_lo[0:M, m], h32[0:M, m % 2], h_hi[0:M, m], ALU.subtract).then_inc(s_hlo, 1)

                for m in range(FC):
                    M = FM[m]
                    dve.wait_ge(s_sg, gi * FC + m + 1)
                    dve.wait_ge(s_pup, gi * FC + m + 1)
                    if m >= 2:
                        dve.wait_ge(s_hlo, gi * FC + m - 1)
                    V_.scalar_tensor_tensor(out=h32[0:M, m % 2], in0=sg[0:M, m % 2], scalar=f_hf[0:M, 0:1],
                                            in1=U[m % 2][0:M, :], op0=ALU.mult, op1=ALU.mult).then_inc(s_h, 1)
                    if m:
                        low(m - 1)
                    if m in SCORES:
                        n = m // 2
                        dve.wait_ge(s_psc, gi * GT + n + 1)
                        V_.tensor_tensor(probs[:, :], B[1][:, 0:HD],
                                         mask[:, :, :].rearrange("p h c -> p (h c)"), ALU.mult).then_inc(s_pr, 1)
                    if m in NEXT_T and not last:
                        xt_low(1 - g, NEXT_T[m], gi * GT + GT + NEXT_T[m] + 1)
                    if m in SCORES:
                        dve.wait_ge(s_prh, gi * GT + m // 2 + 1)
                        V_.tensor_tensor(pr_half[:, m // 2 % 2, 1], probs[:, :], pr_half[:, m // 2 % 2, 0],
                                         ALU.subtract).then_inc(s_prl, 1)
                    if m in RETRIEVE:
                        mix(gi, g, m // 2, RETRIEVE[m])
                        update_state(i, g, m // 2)
                        split_rows(gi, m // 2, RETRIEVE[m])
                low(FC - 1)
                for t in range(GT):
                    dve.wait_ge(s_g, gi * GT + t + 1 + FREE)
                    dve.wait_ge(s_pso, gi * GT + t + 1)
                    dve.wait_ge(s_y[t], 16 * (gi + FREE))
                    V_.scalar_tensor_tensor(out=y_sb[:, t], in0=U[(t + 1) % 2][:, :], scalar=row_out[:, t:t + 1],
                                            in1=g_sb[:, t % 2], op0=ALU.mult, op1=ALU.mult).then_inc(s_y1, 1)
                    dve.wait_ge(s_y1, gi * GT + t + 1 + FREE)
                    V_.tensor_tensor(y_sb[:, t], y_sb[:, t], x_sb[:, g, t], ALU.add).then_inc(s_yr, 1)

            dve.wait_ge(s_mask, 1)
            with dve.Fori(0, NB - 1) as i:
                for g in range(GPB):
                    group(i, g, False)
            for g in range(GPB):
                group(NB - 1, g, g == GPB - 1)

        @block.tensor
        def _(pe):
            T_ = nc.tensor

            def x_transposes(t, n):
                pe.wait_ge(s_xh, n)
                for k in range(KC):
                    ins = T_.transpose(B[2][:, k * P:(k + 1) * P], xhat[:, t, k * P:(k + 1) * P], ident[:, :])
                ins.then_inc(s_xt, 1)

            def look_up(i, u, first):
                b = i * UNR + u
                if not first:
                    pe.wait_ge(s_wst, 2 * (b - UNR + 1))
                for j in range(CG):
                    pe.wait_ge(s_oh, b * CG + j + 1)
                    for pick, bank in ((pick_hi, LUHI[u]), (pick_lo, LULO[u])):
                        for q in range(CG):
                            ins = T_.matmul(bank[QR * q:QR * (q + 1), :], pick[:, j], onehot[:, u, j, q],
                                            start=(j == 0), stop=(j == CG - 1))
                ins.then_inc(s_lu, 1)

            pe.wait_ge(s_pick, 2 * CG)
            pe.wait_ge(s_const, 4)
            for i in range(HEAD):
                for u in range(UNR):
                    look_up(i, u, i == 0)
                    t = (i - 1) * UNR + u
                    if 0 <= t < GT:
                        if t:
                            pe.wait_ge(s_xlo, t)
                        x_transposes(t, t + 1)
            with pe.Fori(HEAD, NBLK // UNR) as i:
                for u in range(UNR):
                    look_up(i, u, False)

            def three(bank, pairs, cols, M=P):
                n = 0
                for k, (sh, sl, mh, ml) in enumerate(pairs):
                    for a, b in ((sh, mh), (sh, ml), (sl, mh)):
                        ins = T_.matmul(bank[0:M, 0:cols], a, b, start=(n == 0), stop=(n == 3 * len(pairs) - 1))
                        n += 1
                return ins

            def sum3(out, ah, al, bh, bl):
                T_.matmul(out, ah, bh, start=True, stop=False)
                T_.matmul(out, ah, bl, start=False, stop=False)
                return T_.matmul(out, al, bh, start=False, stop=True)

            def scores(gi, g, n, t):
                cols = slice(t * P, (t + 1) * P)
                if n == 0:
                    for done in (s_lg, s_vl, s_vbl):
                        pe.wait_ge(done, gi * GT + GT)
                else:
                    pe.wait_ge(s_st, gi * GT + n + 1)
                kt = B[0][:, :].bitcast(F16)
                for s, half in enumerate((qk_hi, qk_lo)):
                    for h in range(NH):
                        ins = T_.transpose(kt[:, (s * NH + h) * D:(s * NH + h + 1) * D], half[:, 1 + h, cols],
                                           ident16[:, :])
                ins.then_inc(s_pkn, 1)
                if n:
                    pe.wait_ge(s_pr, gi * GT + n)
                for h in range(NH):
                    ins = sum3(B[1][:, h * D:(h + 1) * D], qk_hi[:, 1 + h, cols], qk_lo[:, 1 + h, cols],
                               qk_hi[:, 0, cols], qk_lo[:, 0, cols])
                ins.then_inc(s_psc, 1)

            def retrieve(i, g, n, t):
                gi = i * GPB + g
                cols = slice(t * P, (t + 1) * P)
                pe.wait_ge(s_st, gi * GT + n + 1)
                T_.matmul(B[2][:, 0:HD], q32[:, cols], state[:, :], start=True, stop=True)
                pe.wait_ge(s_prl, gi * GT + n + 1)
                for h in range(NH):
                    hc = slice(h * D, (h + 1) * D)
                    ins = sum3(B[3][:, hc], pr_half[:, n % 2, 0, hc], pr_half[:, n % 2, 1, hc],
                               v_hi[:, t, hc], v_lo[:, t, hc])
                ins.then_inc(s_pat, 1)
                if n == GT - 1 and g == GPB - 1:
                    return
                pe.wait_ge(s_kn, gi * GT + n + 1)
                for h in range(NH):
                    hc = slice(h * D, (h + 1) * D)
                    ins = sum3(B[0][:, hc], k_nat[:, n % 2, 0, hc], k_nat[:, n % 2, 1, hc],
                               vb_hi[:, t, hc], vb_lo[:, t, hc])
                ins.then_inc(s_pu, 1)

            def blend(gi, n):
                pe.wait_ge(s_rs, (gi * GT + n + 1) * NRS)
                for s in range(2):
                    ins = T_.transpose(B[3][:, :].bitcast(F16)[:, s * P:(s + 1) * P], mixed_half[:, n % 2, s],
                                       ident16[:, :])
                ins.then_inc(s_pbl, 1)

            def group(i, g, last):
                gi = i * GPB + g
                xh, xl = xt_hi[:, g], xt_lo[:, g]
                pe.wait_ge(s_xlo, gi * GT + GT)
                for j in range(1 + NH):
                    if j >= 2:
                        pe.wait_ge(s_qkl, gi * (1 + NH) + j - 1)
                    elif j == 0:
                        pe.wait_ge(s_st, gi * GT + 1)
                    three(B[j % 2], [(a_hi[:, k, j * D:(j + 1) * D], a_lo[:, k, j * D:(j + 1) * D],
                                      xh[:, k], xl[:, k]) for k in range(KC)], GRP).then_inc(s_pqk, 1)
                for t in range(GT):
                    cols = slice(t * P, (t + 1) * P)
                    if t >= 2:
                        pe.wait_ge(s_qkl, gi * (1 + NH) + 1 + t)
                    elif t == 1:
                        pe.wait_ge(s_bl, gi * GT + FREE)
                    three(B[VB[t]], [(xh[:, k, cols], xl[:, k, cols], a_hi[:, k, CV:QKV], a_lo[:, k, CV:QKV])
                                         for k in range(KC)], HD + NH).then_inc(s_pv, 1)
                for m in range(FC):
                    M = FM[m]
                    if m >= 2:
                        pe.wait_ge(s_sg, gi * FC + m - 1)
                    else:
                        pe.wait_ge(s_g, gi * GT + FREE)
                    for off, bank, done in ((0, G[m % 2], s_pg), (W_UP, U[m % 2], s_pup)):
                        if off:
                            if m >= 2:
                                pe.wait_ge(s_h, gi * FC + m - 1)
                            else:
                                pe.wait_ge(s_y1, gi * GT + FREE)
                        w = [off + k * F + m * P for k in range(KC)]
                        three(bank, [(w_hi[:, c:c + M], w_lo[:, c:c + M], xh[:, k], xl[:, k])
                                     for k, c in enumerate(w)], GRP, M).then_inc(done, 1)
                    if m in SCORES:
                        scores(gi, g, m // 2, SCORES[m])
                    if m in BLEND:
                        blend(gi, m // 2 - 1)
                    if m in NEXT_T and not last:
                        pe.wait_ge(s_mix, (gi * GT + m // 2) * NMIX)
                        x_transposes(NEXT_T[m], gi * GT + GT + NEXT_T[m] + 1)
                    if m in RETRIEVE:
                        if m > 1:
                            if not last:
                                pe.wait_ge(s_xlo, gi * GT + GT + m // 2)
                            pe.wait_ge(s_bl, gi * GT + m // 2 + FREE)
                        retrieve(i, g, m // 2, RETRIEVE[m])
                for t in range(GT):
                    cols = slice(t * P, (t + 1) * P)
                    bf, bs = G[(t + 1) % 2], U[(t + 1) % 2]
                    if t >= 2:
                        pe.wait_ge(s_g, gi * GT + t - 1 + FREE)
                    else:
                        pe.wait_ge(s_h, gi * FC + FC - 1 + t)
                    for k in range(FC):
                        K = FM[k]
                        if t == 0:
                            pe.wait_ge(s_hlo, gi * FC + k + 1)
                        c = W_DOWN + k * V
                        hh, hl = h_hi[0:K, k, cols], h_lo[0:K, k, cols]
                        wh, wl = w_hi[0:K, c:c + V], w_lo[0:K, c:c + V]
                        for n, (a, b) in enumerate(((hh, wh), (hh, wl), (hl, wh))):
                            ins = T_.matmul(bf[:, :], a, b, start=(k == 0 and n == 0), stop=(k == FC - 1 and n == 2))
                    ins.then_inc(s_pf, 1)
                    if t >= 2:
                        pe.wait_ge(s_y1, gi * GT + t - 1 + FREE)
                    if t == 0:
                        pe.wait_ge(s_bl, gi * GT + GT + FREE)
                    sum3(bs[:, :], blend_t[:, t, 0], blend_t[:, t, 1], wo_hi[:, :], wo_lo[:, :]).then_inc(s_pso, 1)

            pe.wait_ge(s_mrow, 16)
            T_.matmul(B[3][:, 0:HD], flip[:, :], mask_up.rearrange("p h t -> p (h t)"),
                      start=True, stop=True).then_inc(s_pmask, 1)
            pe.wait_ge(s_wst, 2 * NBLK)
            pe.wait_ge(s_alo, len(LOWS))
            pe.wait_ge(s_id16, 1)
            pe.wait_ge(s_mask, 1)
            with pe.Fori(0, NB - 1) as i:
                for g in range(GPB):
                    group(i, g, False)
            for g in range(GPB):
                group(NB - 1, g, g == GPB - 1)


def kernel(**inputs):
    import numpy as np
    import concourse.bacc as bacc
    from concourse.bass_utils import run_bass_kernel_spmd as run

    a = {k.replace("L0_", ""): np.ascontiguousarray(v) for k, v in inputs.items()}
    B, T, V = a["attn_x"].shape
    F = a["ffn_gate_idx"].shape[0]
    chunks = -(-F // 128)

    down = np.zeros((chunks * 128, V), a["ffn_down_idx"].dtype)
    down[:F] = a["ffn_down_idx"].T
    parts = [w.T.reshape(V // 128, 128, F).transpose(1, 0, 2).reshape(128, -1)
             for w in (a["ffn_gate_idx"], a["ffn_up_idx"])]
    parts.append(down.reshape(chunks, 128, V).transpose(1, 0, 2).reshape(128, -1))
    cols = sum(p.shape[1] for p in parts)
    blocks = -(-cols // 512)
    blocks += -blocks % 3
    idx = np.zeros((128, blocks * 512), down.dtype)
    idx[:, :cols] = np.concatenate(parts, 1)
    idx = idx.reshape(4, 32, blocks, 512).transpose(2, 1, 0, 3)

    arrays = {
        "x": a["attn_x"].reshape(B * T, V), "idx": idx, "lut": a["ffn_lut"],
        "wq": a["attn_Wq"], "wk": a["attn_Wk"], "wv": a["attn_Wv"], "wo": a["attn_Wo"], "wg": a["attn_Wg"],
        "decay_logits": a["attn_decay_logits"], "out_scale": a["attn_out_scale"].reshape(1),
    }
    arrays = {k: np.ascontiguousarray(v) for k, v in arrays.items()}
    nc = bacc.Bacc("TRN2", target_bir_lowering=False, num_devices=1)
    args = [nc.dram_tensor(f"in_{k}", v.shape, mybir.dt.from_np(v.dtype), kind="ExternalInput").ap()
            for k, v in arrays.items()]
    out = nc.dram_tensor("out_y", (B * T, V), F32, kind="ExternalOutput").ap()
    attention_ffn_kernel(nc, *args, out)
    r = run(nc, [{f"in_{k}": v for k, v in arrays.items()}], core_ids=[0])
    return r.results[0]["out_y"].reshape(B, T, V)
```

```python
from contextlib import ExitStack

import concourse.bass as bass
from concourse import mybir

ALU = mybir.AluOpType
ACT = mybir.ActivationFunctionType
AX = mybir.AxisListType
F32 = mybir.dt.float32
F16 = mybir.dt.float16
I32 = mybir.dt.int32
RADD = bass.bass_isa.ReduceOp.add

P = 128
BANK = 512
GT = 4
GRP = GT * P
NLUT = 16
CG = 4
QR = P // CG

XP = 10
WP = 8
FP = 14
TP = 14
QP = -14
SP = -16
HP = -(5 + 2 * WP + XP)

def attention_ffn_kernel(nc, x, idx, lut, wq, wk, wv, wo, wg, decay_logits, out_scale, out):
    NTOK, V = x.shape
    D = wq.shape[1]
    NH = wk.shape[0]
    KC = V // P
    F = 1376
    FC = -(-F // P)
    FM = [min(P, F - m * P) for m in range(FC)]
    T = 1024
    NB = NTOK // T
    GPB = T // GRP
    assert GPB == 2 and KC == 4 and D == P and V == BANK and NH == 3
    NBLK = idx.shape[0]
    UNR = 3
    TURNS = NBLK // UNR
    PEEL = 5
    assert (TURNS - PEEL) % 2 == 0
    HEAD = 4
    OP = [-QP, -QP, -QP - SP, XP]
    W_UP, W_DOWN = KC * F, 2 * KC * F
    assert NBLK % UNR == 0 and NBLK * BANK >= W_DOWN + FC * V
    QKV = (1 + 2 * NH) * D + NH
    CK, CV, CGT = D, (1 + NH) * D, (1 + 2 * NH) * D
    HD = NH * D
    VB = [2, 3, 0, 1]

    with ExitStack() as ctx:
        def sb(name, shape, dt):
            return ctx.enter_context(nc.sbuf_tensor(name, shape, dt))

        def ps(name, dt=F32):
            return ctx.enter_context(nc.psum_tensor(name, [P, BANK], dt))

        def sem(name):
            return ctx.enter_context(nc.semaphore(name))

        w_hi = sb("w_hi", [P, NBLK * BANK], F16)
        w_lo = sb("w_lo", [P, NBLK * BANK], F16)
        a_hi = sb("a_hi", [P, KC, QKV], F16)
        a_lo = sb("a_lo", [P, KC, QKV], F16)
        wo_hi = sb("wo_hi", [P, V], F16)
        wo_lo = sb("wo_lo", [P, V], F16)
        x_sb = sb("x_sb", [P, 2, GT, V], F32)
        xhat = sb("xhat", [P, V], F32)
        xhat_half = sb("xhat_half", [P, GT, 2, V], F16)
        xt = sb("xt", [P, 2, 2 * KC, GRP], F16)
        xt_hi, xt_lo = xt[:, :, 0:KC], xt[:, :, KC:2 * KC]
        n_qk, n_v = 2 * (1 + NH) * GRP // 2, 2 * GT * HD // 2
        attn = sb("attn", [P, n_qk + 2 * n_v], F32)

        def halves(lo, n, **dims):
            return attn[:, lo:lo + n].bitcast(F16).rearrange("p (s j c) -> p s j c", s=2, **dims)

        qk_hi, qk_lo = (halves(0, n_qk, j=1 + NH)[:, s] for s in range(2))
        v_hi, v_lo = (halves(n_qk, n_v, j=GT)[:, s] for s in range(2))
        vb_hi, vb_lo = (halves(n_qk + n_v, n_v, j=GT)[:, s] for s in range(2))
        q32 = sb("q32", [P, GRP], F32)
        state = sb("state", [P, HD], F32)
        faded = sb("faded", [P, HD], F32)
        mixed = sb("mixed", [P, D], F32)
        mixed_half = sb("mixed_half", [P, 2, 2, D], F16)
        mask = sb("mask", [P, NH, P], F32)
        mask_up = faded[:, :].rearrange("p (h t) -> p h t", h=NH)
        fade_s = sb("fade_s", [P, NH], F32)
        flip = mixed
        fade_end = mask[0:NH, 1]
        fade_rows = nc.dram_tensor("fade_rows", [NH, 2 * P], F32, kind="Internal")
        codes16 = nc.dram_tensor("codes16", [NBLK, QR, CG * BANK], F16, kind="Internal")
        fade_t = sb("fade_t", [P, NH], F32)
        fade_tile = sb("fade_tile", [P, NH], F32)
        decay = sb("decay", [P, NH], F32)
        dlog = sb("dlog", [P, NH], F32)
        oscale = sb("oscale", [P, 1], F32)
        fade_q = sb("fade_q", [P, NH], F32)
        fade_v = sb("fade_v", [P, NH], F32)
        nhalf = sb("nhalf", [P, GT], F32)
        WO, LUT = 4, 5
        amax = sb("amax", [P, 6], F32)
        gsum = sb("gsum", [P, 5], F32)
        ebits = sb("ebits", [P, 6], I32)
        up_e = sb("up_e", [P, 6], I32)
        down_e = sb("down_e", [P, 6], I32)
        hf_e = sb("hf_e", [P, 2], I32)
        scale_up = sb("scale_up", [P, 6], I32)
        scale_down = sb("scale_down", [P, 6], I32)
        scale_hf = sb("scale_hf", [P, 2], I32)
        row_max = sb("row_max", [P, 1], F32)
        row_e = sb("row_e", [P, 1], I32)
        row_up = sb("row_up", [P, 1], I32)
        row_down = sb("row_down", [P, 1], I32)
        row_out = sb("row_out", [P, GT], F32)
        stats = sb("stats", [P, GT, 6], F32)
        moments = sb("moments", [P, GT, 2], F32)
        var = sb("var", [P, GT], F32)
        rstd = sb("rstd", [P, GT], F32)
        logit = sb("logit", [P, GT, NH], F32)
        lmax = sb("lmax", [P, GT], F32)
        lsub = sb("lsub", [P, GT, NH], F32)
        lexp = sb("lexp", [P, GT, NH], F32)
        lsum = sb("lsum", [P, GT], F32)
        lrs = sb("lrs", [P, GT], F32)
        gate = sb("gate", [P, GT, NH], F32)
        gate_t = sb("gate_t", [P, GT, NH], F32)
        lutrow = sb("lutrow", [P, NLUT], F32)
        lutcol = sb("lutcol", [P, CG], F32)
        lut_sc = sb("lut_sc", [P, CG], F32)
        lut_hi = sb("lut_hi", [P, CG], F16)
        lut_hi32 = sb("lut_hi32", [P, CG], F32)
        lut_lo32 = sb("lut_lo32", [P, CG], F32)
        pidx = sb("pidx", [P, 1], I32)
        pquad = sb("pquad", [P, 1], I32)
        code = sb("code", [P, CG], F32)
        eye4 = mask[:, 0].rearrange("p (q c) -> p q c", q=CG)
        eye = sb("eye", [P, QR], F32)
        pick_hi = sb("pick_hi", [P, CG, QR], F16)
        pick_lo = sb("pick_lo", [P, CG, QR], F16)

        HB = FC * GRP * 2
        sizes = dict(h_hi=HB, h_lo=HB, sg=2 * 2048, h32=2 * 2048, g=2 * 2048, y=GT * 2048,
                     bl=GRP * 4, kn=GT * HD * 4, ph=2 * HD * 4)
        build = UNR * CG * CG * BANK * 2
        region = sb("region", [P, max(sum(sizes.values()), build) // 4], F32)
        at = {}
        pos = 0
        for k, n in sizes.items():
            at[k] = region[:, pos // 4:(pos + n) // 4]
            pos += n
        h_hi = at["h_hi"].bitcast(F16).rearrange("p (m t) -> p m t", m=FC)
        h_lo = at["h_lo"].bitcast(F16).rearrange("p (m t) -> p m t", m=FC)
        sg = at["sg"].rearrange("p (b t) -> p b t", b=2)
        h32 = at["h32"].rearrange("p (b t) -> p b t", b=2)
        g_sb = at["g"].rearrange("p (b t) -> p b t", b=2)
        y_sb = at["y"].rearrange("p (b t) -> p b t", b=GT)
        blend_t = at["bl"].bitcast(F16).rearrange("p (b s t) -> p b s t", b=GT, s=2)
        k_nat = at["kn"].bitcast(F16).rearrange("p (s j d) -> p s j d", s=2, d=D)
        probs = faded
        pr_half = at["ph"].bitcast(F16).rearrange("p (b s t) -> p b s t", b=2, s=2)
        vb32 = xhat[:, 0:HD]
        n_oh = UNR * CG * CG * BANK // 2
        onehot = region[:, 0:n_oh].bitcast(F16).rearrange("p (u j q c) -> p u j q c", u=UNR, j=CG, q=CG)
        wo32 = q32
        a32 = attn[:, 0:KC * QKV].rearrange("p (k c) -> p k c", k=KC)
        n_ix = CG * BANK // 2
        spare = x_sb[:, 1].rearrange("p t v -> p (t v)")
        codes = [c.bitcast(F16).rearrange("p (q c) -> p q c", q=CG)
                 for c in (attn[:, KC * QKV:KC * QKV + n_ix], spare[:, 0:n_ix], spare[:, n_ix:2 * n_ix])]

        G = [ps("G0"), ps("G1")]
        U = [ps("U0"), ps("U1")]
        B = [ps("B0"), ps("B1"), ps("B2"), ps("B3")]
        LUHI = [G[0], G[1], B[0]]
        LULO = [U[0], U[1], B[1]]

        s_x = [sem("x_in0"), sem("x_in1")]
        s_y = [sem(f"y_out{t}") for t in range(GT)]
        s_first = [sem(f"first_codes{u}") for u in range(UNR)]
        s_idx = [sem(f"codes_in{u}") for u in range(UNR)]
        s_cast = [sem("codes_cast_even"), sem("codes_cast_odd")]
        s_w = sem("qkv_in")
        s_wo = sem("wo_in")
        s_small = sem("lut_in")
        s_par = sem("parameters_in")
        s_const = sem("const_ready")
        s_cstep = sem("const_step")
        s_init = sem("init_step")
        s_sq = sem("squares_ready")
        s_gsum = sem("norms_ready")
        s_lscale = sem("lut_scales_ready")
        s_osc = sem("out_scale_step")
        s_scale = sem("scales_ready")
        s_dec = sem("decay_step")
        s_pow = sem("power_step")
        s_pick = sem("pick_ready")
        s_row = sem("fade_rows_written")
        s_mrow = sem("mask_rows_in")
        s_pmask = sem("mask_in_psum")
        s_mask = sem("mask_ready")
        s_ahi = sem("a_hi_ready")
        s_alo = sem("a_lo_ready")
        s_oh = sem("onehot_ready")
        s_lu = sem("lookup_done")
        s_wst = sem("w_stored")
        s_bn = sem("bn_done")
        s_mv = sem("moments_done")
        s_var = sem("var_done")
        s_rstd = sem("rstd_done")
        s_xh = sem("xhat_ready")
        s_xhi = sem("xhat_hi_ready")
        s_xlo = sem("xhat_lo_ready")
        s_xt = [sem(f"xt_in{t}") for t in range(GT)]
        s_pqk = sem("qk_in_psum")
        s_q32 = sem("q_ready")
        s_qk = sem("qk_hi_ready")
        s_qkl = sem("qk_lo_ready")
        s_pv = sem("v_in_psum")
        s_v = sem("v_hi_ready")
        s_vl = sem("v_lo_ready")
        s_lg = sem("logits_ready")
        s_vb = sem("vb_ready")
        s_vbh = sem("vb_hi_ready")
        s_vbl = sem("vb_lo_ready")
        s_sm = sem("softmax_step")
        s_exp = sem("exp_ready")
        s_kn = sem("k_nat_in")
        s_psc = sem("scores_in_psum")
        s_pr = sem("probs_ready")
        s_prh = sem("probs_hi_ready")
        s_prl = sem("probs_lo_ready")
        s_pat = sem("retrieved_in_psum")
        s_mix = sem("mix_step")
        s_rs = sem("row_scale_step")
        s_pu = sem("update_in_psum")
        s_fade = sem("state_faded")
        s_st = sem("state_ready")
        s_bl = [sem(f"blend_in{t}") for t in range(GT)]
        s_go = sem("transposes_let_go")
        s_pg = sem("gate_in_psum")
        s_pup = sem("up_in_psum")
        s_sg = sem("silu_ready")
        s_h = sem("h_ready")
        s_hhi = sem("h_hi_ready")
        s_hlo = sem("h_lo_ready")
        s_pf = sem("ffn_in_psum")
        s_pso = sem("attn_in_psum")
        s_g = sem("g_ready")
        s_y1 = sem("product_ready")
        s_yr = sem("y_ready")

        x_v = x.rearrange("(n t p) v -> n p t v", t=GT, p=P)
        out_v = out.rearrange("(n t p) v -> n p t v", t=GT, p=P)

        f_up = scale_up[:, :].bitcast(F32)
        f_down = scale_down[:, :].bitcast(F32)
        f_hf = scale_hf[:, :].bitcast(F32)

        SCORES = {0: 3, 2: 2, 4: 1, 6: 0}
        RETRIEVE = {1: 3, 3: 2, 5: 1, 7: 0}
        XHAT = {1: 0, 3: 1, 5: 2, 7: 3}
        SPLIT = {2: 0, 4: 1, 6: 2, 8: 3}
        PARTS = ((0, CK), (CK, CV), (CV, CGT), (CGT, QKV))
        NSM = 6
        NMIX = 2 * NH
        NRS = 8
        LOWS = [(n, k) for n in range(len(PARTS)) for k in range(KC)] + [(WO, 0)]

        FREE = 1

        def row_group(i, g):
            return i * GPB + (GPB - 1 - g)

        block = ctx.enter_context(nc.Block())

        @block.sync
        def _(sp):
            for t in range(GT):
                sp.sem_inc(s_y[t], 16 * FREE)
            sp.dma_start(lutrow[:, :], lut.partition_broadcast(P)).then_inc(s_small, 16)
            for c in range(CG):
                src = lut.rearrange("(j c) -> c j", c=CG)[c]
                sp.dma_start(lutcol[QR * c:QR * (c + 1), :], src.partition_broadcast(QR),
                             allow_slow_non_contiguous=True).then_inc(s_small, 16)
            sp.dma_start(dlog[:, :], decay_logits.partition_broadcast(P)).then_inc(s_par, 16)
            sp.dma_start(oscale[:, :], out_scale.partition_broadcast(P)).then_inc(s_par, 16)
            sp.dma_start(x_sb[:, 0], x_v[row_group(0, 0)]).then_inc(s_x[0], 16)
            sp.dma_start(a32[:, :, 0:D], wq.rearrange("(c p) d -> p c d", p=P)).then_inc(s_w, 16)
            for h in range(NH):
                sp.dma_start(a32[:, :, CK + h * D:CK + (h + 1) * D],
                             wk[h].rearrange("(c p) d -> p c d", p=P)).then_inc(s_w, 16)
                sp.dma_start(a32[:, :, CV + h * D:CV + (h + 1) * D],
                             wv[h].rearrange("(c p) d -> p c d", p=P)).then_inc(s_w, 16)
            sp.dma_start(a32[:, :, CGT:QKV], wg.rearrange("(c p) d -> p c d", p=P)).then_inc(s_w, 16)
            sp.dma_start(wo32[:, :], wo).then_inc(s_wo, 16)

            def transpose(dst, src, done):
                sp.sem_inc(s_go, 1)
                sp.dma_start_transpose(dst, src).then_inc(done, 16)

            def transpose_x(par, t, n):
                sp.wait_ge(s_xlo, n)
                transpose(xt[:, par, :, t * P:(t + 1) * P], xhat_half[:, t].rearrange("p s v -> p (s v)"), s_xt[t])

            def load_codes(i, u):
                b = i * UNR + u
                sp.wait_ge(s_oh, CG * (b - UNR + 1))
                rows = codes16[bass.ds(b, 1)].broadcast_to([CG, QR, CG * BANK])
                sp.dma_start(codes[u].rearrange("p q c -> p (q c)"), rows).then_inc(s_idx[u], 16)

            for i in range(1, PEEL):
                sp.wait_ge(s_cast[i % 2], 16 * ((i + 1) // 2))
                for u in range(UNR):
                    load_codes(i, u)
                    t = (i - 2) * UNR + u - 1
                    if 0 <= t < GT:
                        transpose_x(0, t, t + 1)
            with nc.allow_non_contiguous_dma(reason="384 values, once"):
                sp.wait_ge(s_cstep, 4)
                sp.dma_start(fade_rows[:, P:2 * P], fade_end).then_inc(s_row, 16)
                sp.wait_ge(s_pow, 1)
                sp.dma_start(fade_rows[:, 0:P].rearrange("h t -> t h"), fade_t[:, :]).then_inc(s_row, 16)
                sp.wait_ge(s_row, 32)
                sp.dma_start(mask_up[:, :, :], bass.AP(fade_rows, 1, [[1, P], [2 * P, NH], [1, P]])).then_inc(s_mrow, 16)
            with sp.Fori(0, (TURNS - PEEL) // 2) as k:
                for r in range(2):
                    i = PEEL + 2 * k + r
                    sp.wait_ge(s_cast[(PEEL + r) % 2], 16 * k + 16 * ((PEEL + r + 1) // 2))
                    for u in range(UNR):
                        load_codes(i, u)
            sp.wait_ge(s_oh, CG * NBLK)

            def group(i, g, last):
                gi = i * GPB + g
                if not last:
                    sp.wait_ge(s_yr, gi * GT + FREE)
                    nxt = row_group(i + (g + 1) // GPB, (g + 1) % GPB)
                    sp.dma_start(x_sb[:, 1 - g], x_v[nxt]).then_inc(s_x[1 - g], 16)
                sp.wait_ge(s_qkl, gi * (1 + NH) + 1 + NH)
                for s, half in enumerate((qk_hi, qk_lo)):
                    transpose(k_nat[:, s], half[:, 1:].rearrange("p j t -> p (j t)"), s_kn)
                for m in range(FC):
                    if m in SPLIT and not last:
                        transpose_x(1 - g, SPLIT[m], gi * GT + GT + SPLIT[m] + 1)
                    if m in RETRIEVE:
                        n, t = m // 2, RETRIEVE[m]
                        sp.wait_ge(s_rs, (gi * GT + n + 1) * NRS)
                        transpose(blend_t[:, t], mixed_half[:, n % 2].rearrange("p s d -> p (s d)"), s_bl[t])
                for t in range(GT):
                    sp.wait_ge(s_yr, gi * GT + t + 1 + FREE)
                    sp.dma_start(out_v[row_group(i, g)][:, t], y_sb[:, t]).then_inc(s_y[t], 16)

            with sp.Fori(0, NB - 1) as i:
                for g in range(GPB):
                    group(i, g, False)
            for g in range(GPB):
                group(NB - 1, g, g == GPB - 1)
            for t in range(GT):
                sp.wait_ge(s_y[t], 16 * (NB * GPB + FREE))

        @block.gpsimd
        def _(pool):
            for b in range(UNR):
                rows = idx[b].rearrange("p q c -> p (q c)").unsqueeze(0).broadcast_to([CG, QR, CG * BANK])
                pool.dma_start(codes[b].rearrange("p q c -> p (q c)"), rows).then_inc(s_first[b], 16)
            def cast_codes(i):
                if i > 2:
                    pool.wait_ge(s_idx[UNR - 1], 16 * (i - 2))
                cut = slice(i * UNR, (i + 1) * UNR)
                pool.dma_start(codes16[cut], idx[cut].rearrange("b p q c -> b p (q c)")).then_inc(s_cast[i % 2], 16)

            cast_codes(1)
            nc.gpsimd.iota(pidx[:, :], pattern=[[0, 1]], base=0, channel_multiplier=1).then_inc(s_const, 1)
            nc.gpsimd.memset(eye4, 0.0).then_inc(s_cstep, 1)
            nc.gpsimd.memset(flip[:, :], 0.0).then_inc(s_cstep, 1)
            nc.gpsimd.memset(nhalf[:, :], -0.5).then_inc(s_cstep, 1)
            nc.gpsimd.memset(fade_end, 0.0).then_inc(s_cstep, 1)
            pool.wait_ge(s_cstep, 4)
            nc.gpsimd.affine_select(out=eye4, in_=eye4, compare_op=ALU.not_equal, fill=1.0, base=0,
                                    pattern=[[-QR, CG], [-1, QR]], channel_multiplier=1).then_inc(s_const, 1)
            nc.gpsimd.affine_select(out=flip[:, :], in_=flip[:, :], compare_op=ALU.not_equal, fill=1.0,
                                    base=-(P - 1), pattern=[[1, P]], channel_multiplier=1).then_inc(s_const, 1)
            pool.wait_ge(s_w, 16 * (2 + 2 * NH))
            cast_codes(2)
            pool.wait_ge(s_var, 2)
            nc.gpsimd.tensor_tensor(rstd[:, :], var[:, :], nhalf[:, :], ALU.pow).then_inc(s_rstd, 1)
            nc.gpsimd.iota(fade_s[:, :], pattern=[[0, NH]], base=0, channel_multiplier=1,
                           allow_small_or_imprecise_dtypes=True).then_inc(s_cstep, 1)
            nc.gpsimd.iota(fade_t[:, :], pattern=[[0, NH]], base=P - 1, channel_multiplier=-1,
                           allow_small_or_imprecise_dtypes=True).then_inc(s_cstep, 1)
            nc.gpsimd.memset(fade_tile[:, :], float(P)).then_inc(s_cstep, 1)
            pool.wait_ge(s_dec, 3)
            pool.wait_ge(s_cstep, 7)
            for m in (fade_t, fade_s, fade_tile):
                nc.gpsimd.tensor_tensor(m[:, :], decay[:, :], m[:, :], ALU.pow).then_inc(s_pow, 1)
            cast_codes(3)
            pool.wait_ge(s_sq, 5)
            nc.gpsimd.partition_all_reduce(gsum[:, :], amax[:, 0:5], P, RADD).then_inc(s_gsum, 1)

            def a_low(n, k):
                pool.wait_ge(s_ahi, 2 * n + 2)
                if n == WO:
                    dst, src, high = wo_lo[:, :], wo32[:, :], wo_hi[:, :]
                else:
                    a, b = PARTS[n]
                    dst, src, high = a_lo[:, k, a:b], a32[:, k, a:b], a_hi[:, k, a:b]
                nc.gpsimd.tensor_tensor(dst, src, high, ALU.subtract).then_inc(s_alo, 1)

            lows = list(LOWS)
            for i in range(4, TURNS):
                cast_codes(i)
                if i > 5:
                    for n, k in lows[:4]:
                        a_low(n, k)
                    lows = lows[4:]

            def group(i, g):
                gi = i * GPB + g
                pool.wait_ge(s_var, 2 * gi + 4)
                nc.gpsimd.tensor_tensor(rstd[:, :], var[:, :], nhalf[:, :], ALU.pow).then_inc(s_rstd, 1)

            with pool.Fori(0, NB - 1) as i:
                for g in range(GPB):
                    group(i, g)
            group(NB - 1, 0)

        @block.scalar
        def _(act):
            act.sem_inc(s_g, FREE)
            act.wait_ge(s_par, 32)
            nc.scalar.activation(decay[:, :], dlog[:, :], ACT.Exp, scale=-1.0).then_inc(s_dec, 1)

            def x_high(t, n):
                act.wait_ge(s_xh, n)
                nc.scalar.activation(xhat_half[:, t, 0], xhat[:, :], ACT.Copy).then_inc(s_xhi, 1)

            def square(n):
                if n == 0:
                    act.wait_ge(s_w, 16 * (2 + 2 * NH))
                if n == WO:
                    act.wait_ge(s_wo, 16)
                    src, dst = wo32[:, :], wo_hi[:, :]
                else:
                    src, dst = a32[:, :, slice(*PARTS[n])], a_hi[:, :, slice(*PARTS[n])]
                nc.scalar.activation(dst, src, ACT.Square, accum_out=amax[:, n:n + 1]).then_inc(s_sq, 1)

            def high(n):
                if n == 0:
                    act.wait_ge(s_scale, 2)
                if n == WO:
                    src, dst = wo32[:, :], wo_hi[:, :]
                else:
                    src, dst = a32[:, :, slice(*PARTS[n])], a_hi[:, :, slice(*PARTS[n])]
                nc.scalar.activation(src, src, ACT.Copy, scale=f_up[:, n:n + 1]).then_inc(s_ahi, 1)
                act.wait_ge(s_ahi, 2 * n + 1)
                nc.scalar.activation(dst, src, ACT.Copy).then_inc(s_ahi, 1)

            def store(i, u):
                b = i * UNR + u
                col = bass.ds(b * BANK, BANK)
                act.wait_ge(s_lu, b + 1)
                nc.scalar.activation(w_hi[:, col], LUHI[u][:, :], ACT.Copy).then_inc(s_wst, 1)
                nc.scalar.activation(w_lo[:, col], LULO[u][:, :], ACT.Copy).then_inc(s_wst, 1)

            for i in range(HEAD):
                for u in range(UNR):
                    store(i, u)
                    t = (i - 1) * UNR + u
                    if 0 <= t < GT:
                        x_high(t, t + 1)
                    if i * UNR + u <= WO:
                        square(i * UNR + u)
                    if i == HEAD - 1:
                        high(u)
                        if u == UNR - 1:
                            high(UNR)
                            high(WO)
            with act.Fori(HEAD, TURNS) as i:
                for u in range(UNR):
                    store(i, u)
            act.wait_ge(s_pmask, 1)
            nc.scalar.activation(mask[:, :, :].rearrange("p h t -> p (h t)"), B[3][:, 0:HD], ACT.Copy,
                                 scale=2.0 ** SP).then_inc(s_mask, 1)

            def group(i, g, last):
                gi = i * GPB + g
                for j in range(1 + NH):
                    act.wait_ge(s_pqk, gi * (1 + NH) + j + 1)
                    if j == 0:
                        nc.scalar.activation(q32[:, :], B[0][:, :], ACT.Copy, scale=2.0 ** QP).then_inc(s_q32, 1)
                    nc.scalar.activation(qk_hi[:, j], B[j % 2][:, :], ACT.Copy, scale=2.0 ** QP).then_inc(s_qk, 1)
                for t in range(GT):
                    act.wait_ge(s_pv, gi * GT + t + 1)
                    nc.scalar.activation(v_hi[:, t], B[VB[t]][:, 0:HD], ACT.Copy, scale=2.0 ** QP).then_inc(s_v, 1)
                    nc.scalar.activation(logit[:, t], B[VB[t]][:, HD:HD + NH], ACT.Copy,
                                         scale=f_down[:, 3:4]).then_inc(s_lg, 1)
                    act.wait_ge(s_vb, gi * GT + t + 1)
                    nc.scalar.activation(vb_hi[:, t], vb32[:, :], ACT.Copy).then_inc(s_vbh, 1)
                act.wait_ge(s_sm, gi * NSM + 2)
                nc.scalar.activation(lexp[:, :, :], lsub[:, :, :], ACT.Exp).then_inc(s_exp, 1)
                for m in range(FC):
                    M = FM[m]
                    act.wait_ge(s_pg, gi * FC + m + 1)
                    if m >= 2:
                        act.wait_ge(s_h, gi * FC + m - 1)
                    nc.scalar.activation(sg[0:M, m % 2], G[m % 2][0:M, :], ACT.Silu,
                                         scale=f_down[0:M, LUT:LUT + 1]).then_inc(s_sg, 1)
                    act.wait_ge(s_h, gi * FC + m + 1)
                    nc.scalar.activation(h_hi[0:M, m], h32[0:M, m % 2], ACT.Copy).then_inc(s_hhi, 1)
                    if m in SCORES:
                        n = m // 2
                        act.wait_ge(s_pr, gi * GT + n + 1)
                        nc.scalar.activation(pr_half[:, n % 2, 0], probs[:, :], ACT.Copy).then_inc(s_prh, 1)
                    if m in XHAT and not last:
                        x_high(XHAT[m], gi * GT + GT + XHAT[m] + 1)
                for t in range(GT):
                    act.wait_ge(s_pf, gi * GT + t + 1)
                    if t >= 2:
                        act.wait_ge(s_y1, gi * GT + t - 1 + FREE)
                    nc.scalar.activation(g_sb[:, t % 2], G[(t + 1) % 2][:, :], ACT.Silu,
                                         scale=f_hf[:, 1:2]).then_inc(s_g, 1)

            with act.Fori(0, NB - 1) as i:
                for g in range(GPB):
                    group(i, g, False)
            for g in range(GPB):
                group(NB - 1, g, g == GPB - 1)

        @block.vector
        def _(dve):
            V_ = nc.vector
            dve.sem_inc(s_y1, FREE)
            dve.sem_inc(s_yr, FREE)
            init = [0]

            def step(ins):
                init[0] += 1
                ins.then_inc(s_init, 1)
                dve.wait_ge(s_init, init[0])

            def norm(par, loads, gi, t0=0):
                def aggregate(t):
                    V_.bn_aggr(moments[:, t], stats[:, t]).then_inc(s_mv, 1)

                def variance(a, b):
                    V_.tensor_scalar(var[:, a:b], moments[:, a:b, 1], 1e-5, 2.0 ** (-2 * XP), ALU.add,
                                     ALU.mult).then_inc(s_var, 1)

                n0 = gi * GT
                dve.wait_ge(s_x[par], loads)
                for t in range(GT):
                    if t >= 2:
                        dve.wait_ge(s_bn, n0 + t - 1)
                    V_.bn_stats(stats[:, t], x_sb[:, par, t]).then_inc(s_bn, 1)
                    if t >= 2:
                        aggregate(t - 2)
                dve.wait_ge(s_bn, n0 + GT)
                dve.wait_ge(s_mv, n0 + 2)
                variance(0, 2)
                aggregate(2)
                aggregate(3)
                dve.wait_ge(s_mv, n0 + GT)
                variance(2, 4)

            def xhat_tile(par, gi, t):
                if t == 0:
                    dve.wait_ge(s_rstd, gi + 1)
                else:
                    dve.wait_ge(s_xlo, gi * GT + t)
                V_.tensor_scalar(xhat[:, :], x_sb[:, par, t], moments[:, t, 0:1], rstd[:, t:t + 1],
                                 ALU.subtract, ALU.mult).then_inc(s_xh, 1)

            def x_low(t, n):
                dve.wait_ge(s_xhi, n)
                V_.tensor_tensor(xhat_half[:, t, 1], xhat[:, :], xhat_half[:, t, 0], ALU.subtract).then_inc(s_xlo, 1)

            def compare(i, u, first):
                b = i * UNR + u
                if first:
                    dve.wait_ge(s_first[u], 16)
                else:
                    dve.wait_ge(s_idx[u], 16 * i)
                    dve.wait_ge(s_lu, b - UNR + 1)
                for j in range(CG):
                    V_.tensor_scalar(onehot[:, u, j], codes[u], code[:, j:j + 1], None,
                                     ALU.is_equal).then_inc(s_oh, 1)

            dve.wait_ge(s_const, 1)
            step(V_.tensor_scalar(pquad[:, :], pidx[:, :], 5, None, ALU.logical_shift_right))
            for j in range(CG):
                ins = V_.tensor_scalar(code[:, j:j + 1], pquad[:, :], float(CG * j), None, ALU.add)
                ins.then_inc(s_init, 1)
                init[0] += 1
            dve.wait_ge(s_init, init[0])

            def exponents(src, cols, lo, hi):
                step(V_.tensor_scalar(ebits[:, cols], src.bitcast(I32), 23, None, ALU.logical_shift_right))
                if cols.start == 0:
                    step(V_.tensor_scalar(ebits[:, cols], ebits[:, cols], 127, None, ALU.add))
                    step(V_.tensor_scalar(ebits[:, cols], ebits[:, cols], 1, None, ALU.logical_shift_right))
                step(V_.tensor_scalar(ebits[:, cols], ebits[:, cols], lo, hi, ALU.max, ALU.min))
                up = FP if cols.start == 0 else WP
                step(V_.tensor_scalar(up_e[:, cols], ebits[:, cols], -1.0, 254.0 + up, ALU.mult, ALU.add))

            def down_exponents(cols, up):
                step(V_.tensor_scalar(down_e[:, cols], ebits[:, cols], float(-up - XP), None, ALU.add))

            def shifted(dst, src, done):
                V_.tensor_scalar(dst, src, 23, None, ALU.logical_shift_left).then_inc(done, 1)

            dve.wait_ge(s_const, 3)
            step(V_.tensor_reduce(eye[:, :], eye4.rearrange("p a c -> p c a"), AX.X, ALU.add))
            dve.wait_ge(s_small, 16 * (CG + 1))
            step(V_.tensor_reduce(amax[:, LUT:LUT + 1], lutrow[:, :], AX.X, ALU.max, apply_absolute_value=True))
            exponents(amax[:, LUT:LUT + 1], slice(LUT, LUT + 1), 90.0, 165.0)
            shifted(scale_up[:, LUT:LUT + 1], up_e[:, LUT:LUT + 1], s_lscale)
            dve.wait_ge(s_lscale, 1)

            step(V_.tensor_scalar(lut_sc[:, :], lutcol[:, :], f_up[:, LUT:LUT + 1], None, ALU.mult))
            step(V_.tensor_copy(lut_hi[:, :], lut_sc[:, :]))
            step(V_.tensor_copy(lut_hi32[:, :], lut_hi[:, :]))
            step(V_.tensor_tensor(lut_lo32[:, :], lut_sc[:, :], lut_hi32[:, :], ALU.subtract))
            for j in range(CG):
                V_.tensor_scalar(pick_hi[:, j], eye[:, :], lut_hi32[:, j:j + 1], None, ALU.mult).then_inc(s_pick, 1)
                V_.tensor_scalar(pick_lo[:, j], eye[:, :], lut_lo32[:, j:j + 1], None, ALU.mult).then_inc(s_pick, 1)

            for i in range(HEAD):
                for u in range(UNR):
                    compare(i, u, i == 0)
                    if i == 0 and u == 0:
                        dve.wait_ge(s_dec, 1)
                        V_.tensor_scalar(decay[:, :], decay[:, :], 1.0, None, ALU.add).then_inc(s_dec, 1)
                        dve.wait_ge(s_dec, 2)
                        V_.reciprocal(decay[:, :], decay[:, :]).then_inc(s_dec, 1)
                    if i == 0 and u == 1:
                        norm(0, 16, 0)
                    if i == 0 and u == 2:
                        down_exponents(slice(LUT, LUT + 1), WP)
                        lut_e = ebits[:, LUT:LUT + 1]
                        step(V_.tensor_scalar(hf_e[:, 0:1], lut_e, -1.0, 254.0 + WP + HP, ALU.mult, ALU.add))
                        step(V_.tensor_scalar(hf_e[:, 1:2], lut_e, 3.0, 127.0 - 3 * 127 - 3 * WP - XP - HP,
                                              ALU.mult, ALU.add))
                        shifted(scale_down[:, LUT:LUT + 1], down_e[:, LUT:LUT + 1], s_lscale)
                        shifted(scale_hf[:, :], hf_e[:, :], s_lscale)
                    t = (i - 1) * UNR + u
                    if 0 < t <= GT:
                        x_low(t - 1, t)
                    if 0 <= t < GT:
                        xhat_tile(0, 0, t)
                    if i == HEAD - 2 and u == UNR - 1:
                        dve.wait_ge(s_gsum, 1)
                        exponents(gsum[:, :], slice(0, LUT), 40.0, 200.0)
                        shifted(scale_up[:, 0:LUT], up_e[:, 0:LUT], s_scale)
                        down_exponents(slice(0, LUT), FP)
                        shifted(scale_down[:, 0:LUT], down_e[:, 0:LUT], s_scale)

            with dve.Fori(HEAD, TURNS) as i:
                for u in range(UNR):
                    compare(i, u, False)

            V_.memset(state[:, :], 0.0).then_inc(s_st, 1)
            dve.wait_ge(s_lscale, 3)
            dve.wait_ge(s_par, 32)
            for m, n in enumerate((0, 1, 2, WO)):
                V_.tensor_scalar(oscale[:, :], oscale[:, :], f_down[:, n:n + 1], 2.0 ** OP[m], ALU.mult,
                                 ALU.mult).then_inc(s_osc, 1)
                dve.wait_ge(s_osc, m + 1)
            dve.wait_ge(s_pow, 3)
            V_.tensor_scalar(fade_q[:, :], fade_t[:, :], 2.0 ** SP, None, ALU.mult).then_inc(s_osc, 1)
            V_.tensor_scalar(fade_v[:, :], fade_s[:, :], 2.0 ** QP, None, ALU.mult).then_inc(s_osc, 1)
            dve.wait_ge(s_osc, 6)

            def heads(ap):
                return ap.rearrange("p (h c) -> p h c", h=NH)

            def spread(col):
                return col[:, :].unsqueeze(2).broadcast_to([P, NH, P])

            def softmax(gi):
                n0 = gi * NSM
                wide = lambda ap: ap[:, :].unsqueeze(2).broadcast_to([P, GT, NH])
                dve.wait_ge(s_lg, gi * GT + GT)
                V_.tensor_reduce(lmax[:, :], logit[:, :, :], AX.X, ALU.max).then_inc(s_sm, 1)
                dve.wait_ge(s_sm, n0 + 1)
                V_.tensor_tensor(lsub[:, :, :], logit[:, :, :], wide(lmax), ALU.subtract).then_inc(s_sm, 1)
                dve.wait_ge(s_exp, gi + 1)
                V_.tensor_reduce(lsum[:, :], lexp[:, :, :], AX.X, ALU.add).then_inc(s_sm, 1)
                dve.wait_ge(s_sm, n0 + 3)
                V_.reciprocal(lrs[:, :], lsum[:, :]).then_inc(s_sm, 1)
                dve.wait_ge(s_sm, n0 + 4)
                V_.tensor_tensor(gate[:, :, :], lexp[:, :, :], wide(lrs), ALU.mult).then_inc(s_sm, 1)
                dve.wait_ge(s_sm, n0 + 5)
                V_.tensor_tensor(gate_t[:, :, :], gate[:, :, :],
                                 fade_q[:, :].unsqueeze(1).broadcast_to([P, GT, NH]), ALU.mult).then_inc(s_sm, 1)

            def mix(gi, g, n, t):
                c0 = (gi * GT + n) * NMIX
                dve.wait_ge(s_pat, gi * GT + n + 1)
                if n == 0:
                    dve.wait_ge(s_sm, gi * NSM + NSM)
                else:
                    dve.wait_ge(s_rs, (gi * GT + n) * NRS)
                acc = mixed[:, :]
                V_.tensor_scalar(acc, B[3][:, 0:D], gate[:, t, 0:1], None, ALU.mult).then_inc(s_mix, 1)
                for h in range(1, NH):
                    dve.wait_ge(s_mix, c0 + h)
                    V_.scalar_tensor_tensor(out=acc, in0=B[3][:, h * D:(h + 1) * D], scalar=gate[:, t, h:h + 1],
                                            in1=acc, op0=ALU.mult, op1=ALU.add).then_inc(s_mix, 1)
                for h in range(NH):
                    dve.wait_ge(s_mix, c0 + NH + h)
                    V_.scalar_tensor_tensor(out=acc, in0=B[2][:, h * D:(h + 1) * D], scalar=gate_t[:, t, h:h + 1],
                                            in1=acc, op0=ALU.mult, op1=ALU.add).then_inc(s_mix, 1)

            def split_rows(gi, n, t):
                c0 = (gi * GT + n) * NRS
                dve.wait_ge(s_mix, (gi * GT + n + 1) * NMIX)
                V_.tensor_reduce(row_max[:, :], mixed[:, :], AX.X, ALU.max, apply_absolute_value=True).then_inc(s_rs, 1)
                dve.wait_ge(s_rs, c0 + 1)
                V_.tensor_scalar(row_e[:, :], row_max[:, :].bitcast(I32), 23, None,
                                 ALU.logical_shift_right).then_inc(s_rs, 1)
                dve.wait_ge(s_rs, c0 + 2)
                V_.tensor_scalar(row_e[:, :], row_e[:, :], 30.0, 230.0, ALU.max, ALU.min).then_inc(s_rs, 1)
                dve.wait_ge(s_rs, c0 + 3)
                V_.tensor_scalar(row_up[:, :], row_e[:, :], -2.0 ** 23, (254.0 + TP) * 2.0 ** 23, ALU.mult,
                                 ALU.add).then_inc(s_rs, 1)
                V_.tensor_scalar(row_down[:, :], row_e[:, :], 2.0 ** 23, -TP * 2.0 ** 23, ALU.mult,
                                 ALU.add).then_inc(s_rs, 1)
                dve.wait_ge(s_rs, c0 + 5)
                up = row_up[:, :].bitcast(F32)
                if n >= 2:
                    dve.wait_ge(s_bl[t + 2], 16 * (gi + 1))
                V_.tensor_scalar(mixed_half[:, n % 2, 0], mixed[:, :], up, None, ALU.mult).then_inc(s_rs, 1)
                V_.tensor_scalar(row_out[:, t:t + 1], row_down[:, :].bitcast(F32), oscale[:, 0:1], None,
                                 ALU.mult).then_inc(s_rs, 1)
                dve.wait_ge(s_rs, c0 + 7)
                V_.scalar_tensor_tensor(out=mixed_half[:, n % 2, 1], in0=mixed[:, :], scalar=up,
                                        in1=mixed_half[:, n % 2, 0], op0=ALU.mult, op1=ALU.subtract).then_inc(s_rs, 1)

            def update_state(i, g, n):
                if n == GT - 1 and g == GPB - 1:
                    dve.wait_ge(s_pat, (i * GPB + g) * GT + n + 1)
                    V_.memset(state[:, :], 0.0).then_inc(s_st, 1)
                    return
                k = i * (GPB * GT - 1) + g * GT + n
                dve.wait_ge(s_st, i * GPB * GT + g * GT + n + 1)
                dve.wait_ge(s_prl, i * GPB * GT + g * GT + n + 1)
                V_.tensor_tensor(heads(faded[:, :]), heads(state[:, :]), spread(fade_tile), ALU.mult).then_inc(s_fade, 1)
                dve.wait_ge(s_fade, k + 1)
                dve.wait_ge(s_pu, k + 1)
                V_.tensor_tensor(state[:, :], B[0][:, 0:HD], faded[:, :], ALU.add).then_inc(s_st, 1)

            def group(i, g, last):
                gi = i * GPB + g
                for j in range(1 + NH):
                    if j == 0:
                        dve.wait_ge(s_q32, gi + 1)
                    dve.wait_ge(s_qk, gi * (1 + NH) + j + 1)
                    V_.scalar_tensor_tensor(out=qk_lo[:, j], in0=B[j % 2][:, :], scalar=2.0 ** QP, in1=qk_hi[:, j],
                                            op0=ALU.mult, op1=ALU.subtract).then_inc(s_qkl, 1)
                if not last:
                    norm(1 - g, 16 * (i + g) + 16, gi + 1)
                for t in range(GT):
                    dve.wait_ge(s_lg, gi * GT + t + 1)
                    if t:
                        dve.wait_ge(s_vbl, gi * GT + t)
                    V_.tensor_tensor(heads(vb32[:, :]), heads(B[VB[t]][:, 0:HD]), spread(fade_v),
                                     ALU.mult).then_inc(s_vb, 1)
                    V_.scalar_tensor_tensor(out=v_lo[:, t], in0=B[VB[t]][:, 0:HD], scalar=2.0 ** QP, in1=v_hi[:, t],
                                            op0=ALU.mult, op1=ALU.subtract).then_inc(s_vl, 1)
                    dve.wait_ge(s_vbh, gi * GT + t + 1)
                    V_.tensor_tensor(vb_lo[:, t], vb32[:, :], vb_hi[:, t], ALU.subtract).then_inc(s_vbl, 1)
                softmax(gi)

                def low(m):
                    M = FM[m]
                    dve.wait_ge(s_hhi, gi * FC + m + 1)
                    V_.tensor_tensor(h_lo[0:M, m], h32[0:M, m % 2], h_hi[0:M, m], ALU.subtract).then_inc(s_hlo, 1)

                for m in range(FC):
                    M = FM[m]
                    dve.wait_ge(s_sg, gi * FC + m + 1)
                    dve.wait_ge(s_pup, gi * FC + m + 1)
                    if m >= 2:
                        dve.wait_ge(s_hlo, gi * FC + m - 1)
                    V_.scalar_tensor_tensor(out=h32[0:M, m % 2], in0=sg[0:M, m % 2], scalar=f_hf[0:M, 0:1],
                                            in1=U[m % 2][0:M, :], op0=ALU.mult, op1=ALU.mult).then_inc(s_h, 1)
                    if m:
                        low(m - 1)
                    if m in SCORES:
                        n = m // 2
                        dve.wait_ge(s_psc, gi * GT + n + 1)
                        dve.wait_ge(s_st, gi * GT + n + 1)
                        V_.tensor_tensor(probs[:, :], B[1][:, 0:HD],
                                         mask[:, :, :].rearrange("p h c -> p (h c)"), ALU.mult).then_inc(s_pr, 1)
                    if m in XHAT and not last:
                        dve.wait_ge(s_xt[XHAT[m]], 16 * (gi + 1))
                        xhat_tile(1 - g, gi + 1, XHAT[m])
                    if m in SPLIT and not last:
                        x_low(SPLIT[m], gi * GT + GT + SPLIT[m] + 1)
                    if m in SCORES:
                        dve.wait_ge(s_prh, gi * GT + m // 2 + 1)
                        V_.tensor_tensor(pr_half[:, m // 2 % 2, 1], probs[:, :], pr_half[:, m // 2 % 2, 0],
                                         ALU.subtract).then_inc(s_prl, 1)
                    if m in RETRIEVE:
                        mix(gi, g, m // 2, RETRIEVE[m])
                        update_state(i, g, m // 2)
                        split_rows(gi, m // 2, RETRIEVE[m])
                low(FC - 1)
                for t in range(GT):
                    dve.wait_ge(s_g, gi * GT + t + 1 + FREE)
                    dve.wait_ge(s_pso, gi * GT + t + 1)
                    dve.wait_ge(s_y[t], 16 * (gi + FREE))
                    V_.scalar_tensor_tensor(out=y_sb[:, t], in0=U[(t + 1) % 2][:, :], scalar=row_out[:, t:t + 1],
                                            in1=g_sb[:, t % 2], op0=ALU.mult, op1=ALU.mult).then_inc(s_y1, 1)
                    dve.wait_ge(s_y1, gi * GT + t + 1 + FREE)
                    V_.tensor_tensor(y_sb[:, t], y_sb[:, t], x_sb[:, g, t], ALU.add).then_inc(s_yr, 1)

            dve.wait_ge(s_mask, 1)
            with dve.Fori(0, NB - 1) as i:
                for g in range(GPB):
                    group(i, g, False)
            for g in range(GPB):
                group(NB - 1, g, g == GPB - 1)

        @block.tensor
        def _(pe):
            T_ = nc.tensor

            def look_up(i, u, first):
                b = i * UNR + u
                if not first:
                    pe.wait_ge(s_wst, 2 * (b - UNR + 1))
                for j in range(CG):
                    pe.wait_ge(s_oh, b * CG + j + 1)
                    for pick, bank in ((pick_hi, LUHI[u]), (pick_lo, LULO[u])):
                        for q in range(CG):
                            ins = T_.matmul(bank[QR * q:QR * (q + 1), :], pick[:, j], onehot[:, u, j, q],
                                            start=(j == 0), stop=(j == CG - 1))
                ins.then_inc(s_lu, 1)

            pe.wait_ge(s_pick, 2 * CG)
            for i in range(HEAD):
                for u in range(UNR):
                    look_up(i, u, i == 0)
            with pe.Fori(HEAD, TURNS) as i:
                for u in range(UNR):
                    look_up(i, u, False)

            def three(bank, pairs, cols, M=P):
                n = 0
                for k, (sh, sl, mh, ml) in enumerate(pairs):
                    for a, b in ((sh, mh), (sh, ml), (sl, mh)):
                        ins = T_.matmul(bank[0:M, 0:cols], a, b, start=(n == 0), stop=(n == 3 * len(pairs) - 1))
                        n += 1
                return ins

            def sum3(out, ah, al, bh, bl):
                T_.matmul(out, ah, bh, start=True, stop=False)
                T_.matmul(out, ah, bl, start=False, stop=False)
                return T_.matmul(out, al, bh, start=False, stop=True)

            def scores(gi, g, n, t):
                cols = slice(t * P, (t + 1) * P)
                if n == 0:
                    for done in (s_lg, s_vl, s_vbl):
                        pe.wait_ge(done, gi * GT + GT)
                else:
                    pe.wait_ge(s_pr, gi * GT + n)
                for h in range(NH):
                    ins = sum3(B[1][:, h * D:(h + 1) * D], qk_hi[:, 1 + h, cols], qk_lo[:, 1 + h, cols],
                               qk_hi[:, 0, cols], qk_lo[:, 0, cols])
                ins.then_inc(s_psc, 1)

            def retrieve(i, g, n, t):
                gi = i * GPB + g
                cols = slice(t * P, (t + 1) * P)
                if n:
                    pe.wait_ge(s_mix, (gi * GT + n) * NMIX)
                pe.wait_ge(s_st, gi * GT + n + 1)
                T_.matmul(B[2][:, 0:HD], q32[:, cols], state[:, :], start=True, stop=True)
                pe.wait_ge(s_prl, gi * GT + n + 1)
                for h in range(NH):
                    hc = slice(h * D, (h + 1) * D)
                    ins = sum3(B[3][:, hc], pr_half[:, n % 2, 0, hc], pr_half[:, n % 2, 1, hc],
                               v_hi[:, t, hc], v_lo[:, t, hc])
                ins.then_inc(s_pat, 1)
                if n == GT - 1 and g == GPB - 1:
                    return
                if n == 0:
                    pe.wait_ge(s_kn, 32 * (gi + 1))
                for h in range(NH):
                    hc = slice(h * D, (h + 1) * D)
                    ins = sum3(B[0][:, hc], k_nat[:, 0, h * GT + t], k_nat[:, 1, h * GT + t],
                               vb_hi[:, t, hc], vb_lo[:, t, hc])
                ins.then_inc(s_pu, 1)

            def group(i, g, last):
                gi = i * GPB + g
                xh, xl = xt_hi[:, g], xt_lo[:, g]
                for t in range(GT):
                    pe.wait_ge(s_xt[t], 16 * (gi + 1))
                for j in range(1 + NH):
                    if j >= 2:
                        pe.wait_ge(s_qkl, gi * (1 + NH) + j - 1)
                    elif j == 0:
                        pe.wait_ge(s_st, gi * GT + 1)
                    three(B[j % 2], [(a_hi[:, k, j * D:(j + 1) * D], a_lo[:, k, j * D:(j + 1) * D],
                                      xh[:, k], xl[:, k]) for k in range(KC)], GRP).then_inc(s_pqk, 1)
                for t in range(GT):
                    cols = slice(t * P, (t + 1) * P)
                    if t >= 2:
                        pe.wait_ge(s_qkl, gi * (1 + NH) + 1 + t)
                    three(B[VB[t]], [(xh[:, k, cols], xl[:, k, cols], a_hi[:, k, CV:QKV], a_lo[:, k, CV:QKV])
                                         for k in range(KC)], HD + NH).then_inc(s_pv, 1)
                for m in range(FC):
                    M = FM[m]
                    if m >= 2:
                        pe.wait_ge(s_sg, gi * FC + m - 1)
                    else:
                        pe.wait_ge(s_g, gi * GT + FREE)
                    for off, bank, done in ((0, G[m % 2], s_pg), (W_UP, U[m % 2], s_pup)):
                        if off:
                            if m >= 2:
                                pe.wait_ge(s_h, gi * FC + m - 1)
                            else:
                                pe.wait_ge(s_y1, gi * GT + FREE)
                        w = [off + k * F + m * P for k in range(KC)]
                        three(bank, [(w_hi[:, c:c + M], w_lo[:, c:c + M], xh[:, k], xl[:, k])
                                     for k, c in enumerate(w)], GRP, M).then_inc(done, 1)
                    if m in SCORES:
                        scores(gi, g, m // 2, SCORES[m])
                    if m in RETRIEVE:
                        retrieve(i, g, m // 2, RETRIEVE[m])
                for t in range(GT):
                    cols = slice(t * P, (t + 1) * P)
                    bf, bs = G[(t + 1) % 2], U[(t + 1) % 2]
                    if t >= 2:
                        pe.wait_ge(s_g, gi * GT + t - 1 + FREE)
                    else:
                        pe.wait_ge(s_h, gi * FC + FC - 1 + t)
                    for k in range(FC):
                        K = FM[k]
                        if t == 0:
                            pe.wait_ge(s_hlo, gi * FC + k + 1)
                        c = W_DOWN + k * V
                        hh, hl = h_hi[0:K, k, cols], h_lo[0:K, k, cols]
                        wh, wl = w_hi[0:K, c:c + V], w_lo[0:K, c:c + V]
                        for n, (a, b) in enumerate(((hh, wh), (hh, wl), (hl, wh))):
                            ins = T_.matmul(bf[:, :], a, b, start=(k == 0 and n == 0), stop=(k == FC - 1 and n == 2))
                    ins.then_inc(s_pf, 1)
                    if t >= 2:
                        pe.wait_ge(s_y1, gi * GT + t - 1 + FREE)
                    pe.wait_ge(s_bl[t], 16 * (gi + 1))
                    sum3(bs[:, :], blend_t[:, t, 0], blend_t[:, t, 1], wo_hi[:, :], wo_lo[:, :]).then_inc(s_pso, 1)

            pe.wait_ge(s_mrow, 16)
            T_.matmul(B[3][:, 0:HD], flip[:, :], mask_up.rearrange("p h t -> p (h t)"),
                      start=True, stop=True).then_inc(s_pmask, 1)
            pe.wait_ge(s_wst, 2 * NBLK)
            pe.wait_ge(s_alo, len(LOWS))
            pe.wait_ge(s_mask, 1)
            with pe.Fori(0, NB - 1) as i:
                for g in range(GPB):
                    group(i, g, False)
            for g in range(GPB):
                group(NB - 1, g, g == GPB - 1)


def kernel(**inputs):
    import numpy as np
    import concourse.bacc as bacc
    from concourse.bass_utils import run_bass_kernel_spmd as run

    a = {k.replace("L0_", ""): np.ascontiguousarray(v) for k, v in inputs.items()}
    B, T, V = a["attn_x"].shape
    F = a["ffn_gate_idx"].shape[0]
    chunks = -(-F // 128)

    down = np.zeros((chunks * 128, V), a["ffn_down_idx"].dtype)
    down[:F] = a["ffn_down_idx"].T
    parts = [w.T.reshape(V // 128, 128, F).transpose(1, 0, 2).reshape(128, -1)
             for w in (a["ffn_gate_idx"], a["ffn_up_idx"])]
    parts.append(down.reshape(chunks, 128, V).transpose(1, 0, 2).reshape(128, -1))
    cols = sum(p.shape[1] for p in parts)
    blocks = -(-cols // 512)
    blocks += -blocks % 3
    idx = np.zeros((128, blocks * 512), down.dtype)
    idx[:, :cols] = np.concatenate(parts, 1)
    idx = idx.reshape(4, 32, blocks, 512).transpose(2, 1, 0, 3)

    arrays = {
        "x": a["attn_x"].reshape(B * T, V), "idx": idx, "lut": a["ffn_lut"],
        "wq": a["attn_Wq"], "wk": a["attn_Wk"], "wv": a["attn_Wv"], "wo": a["attn_Wo"], "wg": a["attn_Wg"],
        "decay_logits": a["attn_decay_logits"], "out_scale": a["attn_out_scale"].reshape(1),
    }
    arrays = {k: np.ascontiguousarray(v) for k, v in arrays.items()}
    nc = bacc.Bacc("TRN2", target_bir_lowering=False, num_devices=1)
    args = [nc.dram_tensor(f"in_{k}", v.shape, mybir.dt.from_np(v.dtype), kind="ExternalInput").ap()
            for k, v in arrays.items()]
    out = nc.dram_tensor("out_y", (B * T, V), F32, kind="ExternalOutput").ap()
    attention_ffn_kernel(nc, *args, out)
    r = run(nc, [{f"in_{k}": v for k, v in arrays.items()}], core_ids=[0])
    return r.results[0]["out_y"].reshape(B, T, V)
```
